# Optimizing a Trainium2 kernel written in Bass

```python
import numpy as np
import jax
import jax.numpy as jnp

def _softmax(x, axis=-1):
    return jax.nn.softmax(x, axis=axis)

def _gelu(x):
    return jax.nn.gelu(x, approximate=True)

def _silu(x):
    return jax.nn.silu(x)

def _sigmoid(x):
    return jax.nn.sigmoid(x)

def _layernorm(x, axis=-1, eps=1e-05):
    m = jnp.mean(x, axis=axis, keepdims=True)
    v = jnp.var(x, axis=axis, keepdims=True)
    return (x - m) / jnp.sqrt(v + eps)

def _scatter_add(tgt, idx, src, axis=0):
    return tgt.at[idx].add(src)

def _segment_sum(src, seg, n):
    return jax.ops.segment_sum(src, seg, n)
kernel_name = 'mk_sandwich_d2_jaxref_r8_005c8e'

def setup_inputs(seed: int=0):
    np.random.seed(seed)
    _w = jnp.asarray

    def _L0_attn_setup():
        import math
        import jax, jax.numpy as jnp
        import numpy as np
        NUM_HEADS = 32
        HIDDEN = 512
        HEAD_DIM = HIDDEN // NUM_HEADS
        NEG_INF = -1e+30

        def _alibi_slopes(n: int) -> jnp.ndarray:
            cp2 = 2 ** math.floor(math.log2(n))
            base = 2.0 ** (-2.0 ** (-(math.log2(cp2) - 3)))
            slopes = base ** np.arange(1, cp2 + 1, dtype=np.float64)
            if cp2 != n:
                extra_base = 2.0 ** (-2.0 ** (-(math.log2(2 * cp2) - 3)))
                rem = min(cp2, n - cp2)
                extra = extra_base ** np.arange(1, 1 + 2 * rem, 2, dtype=np.float64)
                slopes = np.concatenate([slopes, extra])
            return jnp.asarray(slopes, dtype=jnp.float32)
        key = jax.random.key(seed)
        k1, k2, k3 = jax.random.split(key, 3)
        B, S = (2, 256)
        hidden_states = jax.random.normal(k1, (B, S, HIDDEN), dtype=jnp.float32)
        Wqkv = jax.random.normal(k2, (HIDDEN, NUM_HEADS * HEAD_DIM + 2 * HEAD_DIM), dtype=jnp.float32) * 0.02
        Wo = jax.random.normal(k3, (HIDDEN, HIDDEN), dtype=jnp.float32) * 0.02
        return {'hidden_states': hidden_states, 'Wqkv': Wqkv, 'Wo': Wo}
    _L0_attn_in = _L0_attn_setup()

    def _L0_ffn_setup():
        import jax, jax.numpy as jnp
        import numpy as np
        HID = 512
        INTER = 1376
        BITS = 4
        PACK = 8
        MAXQ = 15
        GROUP = 128

        def _dequant(qweight, scales, qzeros, g_idx):
            shifts = jnp.arange(PACK, dtype=jnp.uint32) * BITS
            qw = qweight.astype(jnp.uint32)
            w = (qw[:, None, :] >> shifts[None, :, None] & MAXQ).reshape(-1, qweight.shape[1])
            qz = qzeros.astype(jnp.uint32)
            z = ((qz[:, :, None] >> shifts[None, None, :] & MAXQ) + 1).reshape(qzeros.shape[0], -1)
            s = scales[g_idx]
            return (w.astype(scales.dtype) - z[g_idx].astype(scales.dtype)) * s
        key = jax.random.key(seed)
        ks = jax.random.split(key, 16)

        def qw(k, K, N):
            return jax.random.randint(k, (K // PACK, N), 0, 2147483647, dtype=jnp.int32)

        def qz(k, G, N):
            return jax.random.randint(k, (G, N // PACK), 0, 2147483647, dtype=jnp.int32)

        def sc(k, G, N):
            return jax.random.uniform(k, (G, N), jnp.float32, 0.001, 0.01)
        Gk = HID // GROUP
        Gd = INTER // GROUP
        return {'x': jax.random.normal(ks[0], (4, 256, HID), jnp.float32), 'gate_qweight': qw(ks[1], HID, INTER), 'gate_scales': sc(ks[2], Gk, INTER), 'gate_qzeros': qz(ks[3], Gk, INTER), 'gate_g_idx': (jnp.arange(HID) // GROUP).astype(jnp.int32), 'up_qweight': qw(ks[4], HID, INTER), 'up_scales': sc(ks[5], Gk, INTER), 'up_qzeros': qz(ks[6], Gk, INTER), 'up_g_idx': (jnp.arange(HID) // GROUP).astype(jnp.int32), 'down_qweight': qw(ks[7], INTER, HID), 'down_scales': sc(ks[8], Gd, HID), 'down_qzeros': qz(ks[9], Gd, HID), 'down_g_idx': (jnp.arange(INTER) // GROUP).astype(jnp.int32)}
    _L0_ffn_in = _L0_ffn_setup()

    def _L1_attn_setup():
        import jax, jax.numpy as jnp
        import numpy as np
        BH = 32
        BW = 32
        key = jax.random.key(seed)
        k1, k2, k3, k4 = jax.random.split(key, 4)
        B, S, K, N = (2, 256, 512, 512)
        data = jax.random.normal(k1, (B, S, K), dtype=jnp.float32)
        weight = jax.random.normal(k2, (N, K), dtype=jnp.float32) * 0.02
        bias = jax.random.normal(k3, (N,), dtype=jnp.float32) * 0.02
        Nb, Kb = (N // BH, K // BW)
        block_on = jax.random.uniform(k4, (Nb, Kb)) < 0.3
        mask = jnp.repeat(jnp.repeat(block_on, BH, axis=0), BW, axis=1).astype(jnp.int32)
        return {'data': data, 'mask': mask, 'weight': weight, 'bias': bias}
    _L1_attn_in = _L1_attn_setup()

    def _L1_ffn_setup():
        import math
        import jax, jax.numpy as jnp
        import numpy as np
        SCALING = 16.0 / 32.0

        def real_fourier_orthogonal_multiply(c):
            n = c.shape[-1]
            sqrt_n = math.sqrt(n)
            pair_scale = math.sqrt(n / 2.0)
            max_f = (n - 1) // 2
            work = c.astype(jnp.float32)
            dc = (work[..., 0] * sqrt_n)[..., None].astype(jnp.complex64)
            cos = work[..., 1:1 + 2 * max_f:2] * pair_scale
            sin = work[..., 2:2 + 2 * max_f:2] * pair_scale
            mid = (cos - 1j * sin).astype(jnp.complex64)
            parts = [dc, mid]
            if n % 2 == 0:
                parts.append((work[..., -1] * sqrt_n)[..., None].astype(jnp.complex64))
            spectrum = jnp.concatenate(parts, axis=-1)
            return jnp.fft.irfft(spectrum, n=n, axis=-1).astype(c.dtype)
        key = jax.random.key(seed)
        ks = jax.random.split(key, 9)
        B, S, D_in, D_out, R0, R1, E = (4, 256, 512, 512, 32, 8, 3)
        x = jax.random.normal(ks[0], (B, S, D_in), dtype=jnp.float32)
        W_base = jax.random.normal(ks[1], (D_out, D_in), dtype=jnp.float32) * 0.02
        b_base = jax.random.normal(ks[2], (D_out,), dtype=jnp.float32) * 0.02
        enc0 = jax.random.normal(ks[3], (R0, D_in), dtype=jnp.float32) * 0.02
        enc1 = jax.random.normal(ks[4], (R1, D_in), dtype=jnp.float32) * 0.02
        coefs0 = jax.random.normal(ks[5], (E, D_out, R0), dtype=jnp.float32) * 0.02
        coefs1 = jax.random.normal(ks[6], (E, D_out, R1), dtype=jnp.float32) * 0.02
        mask0 = jax.random.randint(ks[7], (E, D_out, R0), 0, 2).astype(bool)
        mask1 = jax.random.randint(ks[8], (E, D_out, R1), 0, 2).astype(bool)
        return dict(x=x, W_base=W_base, b_base=b_base, enc0=enc0, enc1=enc1, coefs0=coefs0, coefs1=coefs1, mask0=mask0, mask1=mask1)
    _L1_ffn_in = _L1_ffn_setup()
    _d = {'L0_attn_hidden_states': _L0_attn_in['hidden_states'], 'L0_attn_Wqkv': _L0_attn_in['Wqkv'], 'L0_attn_Wo': _L0_attn_in['Wo'], 'L0_ffn_gate_qweight': _L0_ffn_in['gate_qweight'], 'L0_ffn_gate_scales': _L0_ffn_in['gate_scales'], 'L0_ffn_gate_qzeros': _L0_ffn_in['gate_qzeros'], 'L0_ffn_gate_g_idx': _L0_ffn_in['gate_g_idx'], 'L0_ffn_up_qweight': _L0_ffn_in['up_qweight'], 'L0_ffn_up_scales': _L0_ffn_in['up_scales'], 'L0_ffn_up_qzeros': _L0_ffn_in['up_qzeros'], 'L0_ffn_up_g_idx': _L0_ffn_in['up_g_idx'], 'L0_ffn_down_qweight': _L0_ffn_in['down_qweight'], 'L0_ffn_down_scales': _L0_ffn_in['down_scales'], 'L0_ffn_down_qzeros': _L0_ffn_in['down_qzeros'], 'L0_ffn_down_g_idx': _L0_ffn_in['down_g_idx'], 'L1_attn_mask': _L1_attn_in['mask'], 'L1_attn_weight': _L1_attn_in['weight'], 'L1_attn_bias': _L1_attn_in['bias'], 'L1_ffn_W_base': _L1_ffn_in['W_base'], 'L1_ffn_b_base': _L1_ffn_in['b_base'], 'L1_ffn_enc0': _L1_ffn_in['enc0'], 'L1_ffn_enc1': _L1_ffn_in['enc1'], 'L1_ffn_coefs0': _L1_ffn_in['coefs0'], 'L1_ffn_coefs1': _L1_ffn_in['coefs1'], 'L1_ffn_mask0': _L1_ffn_in['mask0'], 'L1_ffn_mask1': _L1_ffn_in['mask1']}
    _x0 = _d['L0_attn_hidden_states']
    _d['L0_attn_hidden_states'] = jax.random.normal(jax.random.fold_in(jax.random.key(seed), 1), (2, 1024, 512), dtype=_x0.dtype)
    del _x0
    return _d

def reference(L0_attn_hidden_states, L0_attn_Wqkv, L0_attn_Wo, L0_ffn_gate_qweight, L0_ffn_gate_scales, L0_ffn_gate_qzeros, L0_ffn_gate_g_idx, L0_ffn_up_qweight, L0_ffn_up_scales, L0_ffn_up_qzeros, L0_ffn_up_g_idx, L0_ffn_down_qweight, L0_ffn_down_scales, L0_ffn_down_qzeros, L0_ffn_down_g_idx, L1_attn_mask, L1_attn_weight, L1_attn_bias, L1_ffn_W_base, L1_ffn_b_base, L1_ffn_enc0, L1_ffn_enc1, L1_ffn_coefs0, L1_ffn_coefs1, L1_ffn_mask0, L1_ffn_mask1):

    def _L0_attn_ref(hidden_states, Wqkv, Wo):
        import math
        import jax, jax.numpy as jnp
        import numpy as np
        NUM_HEADS = 32
        HIDDEN = 512
        HEAD_DIM = HIDDEN // NUM_HEADS
        NEG_INF = -1e+30

        def _alibi_slopes(n: int) -> jnp.ndarray:
            cp2 = 2 ** math.floor(math.log2(n))
            base = 2.0 ** (-2.0 ** (-(math.log2(cp2) - 3)))
            slopes = base ** np.arange(1, cp2 + 1, dtype=np.float64)
            if cp2 != n:
                extra_base = 2.0 ** (-2.0 ** (-(math.log2(2 * cp2) - 3)))
                rem = min(cp2, n - cp2)
                extra = extra_base ** np.arange(1, 1 + 2 * rem, 2, dtype=np.float64)
                slopes = np.concatenate([slopes, extra])
            return jnp.asarray(slopes, dtype=jnp.float32)
        B, S, H = hidden_states.shape
        nH, d = (NUM_HEADS, HEAD_DIM)
        scale = d ** (-0.5)
        qkv = hidden_states @ Wqkv
        q = qkv[..., :nH * d].reshape(B, S, nH, d)
        k = qkv[..., nH * d:nH * d + d]
        v = qkv[..., nH * d + d:]
        scores = jnp.einsum('bqhd,bkd->bhqk', q, k) * scale
        pos_q = jnp.arange(S)[:, None]
        pos_k = jnp.arange(S)[None, :]
        slopes = _alibi_slopes(nH)
        alibi = slopes[:, None, None] * (pos_k - pos_q).astype(jnp.float32)
        causal = pos_k <= pos_q
        scores = jnp.where(causal[None, None], scores + alibi[None], NEG_INF)
        probs = jax.nn.softmax(scores, axis=-1)
        attn = jnp.einsum('bhqk,bkd->bqhd', probs, v).reshape(B, S, H)
        return attn @ Wo

    def _L0_ffn_ref(x, gate_qweight, gate_scales, gate_qzeros, gate_g_idx, up_qweight, up_scales, up_qzeros, up_g_idx, down_qweight, down_scales, down_qzeros, down_g_idx):
        import jax, jax.numpy as jnp
        import numpy as np
        HID = 512
        INTER = 1376
        BITS = 4
        PACK = 8
        MAXQ = 15
        GROUP = 128

        def _dequant(qweight, scales, qzeros, g_idx):
            shifts = jnp.arange(PACK, dtype=jnp.uint32) * BITS
            qw = qweight.astype(jnp.uint32)
            w = (qw[:, None, :] >> shifts[None, :, None] & MAXQ).reshape(-1, qweight.shape[1])
            qz = qzeros.astype(jnp.uint32)
            z = ((qz[:, :, None] >> shifts[None, None, :] & MAXQ) + 1).reshape(qzeros.shape[0], -1)
            s = scales[g_idx]
            return (w.astype(scales.dtype) - z[g_idx].astype(scales.dtype)) * s
        Wg = _dequant(gate_qweight, gate_scales, gate_qzeros, gate_g_idx)
        Wu = _dequant(up_qweight, up_scales, up_qzeros, up_g_idx)
        Wd = _dequant(down_qweight, down_scales, down_qzeros, down_g_idx)
        xf = x.reshape(-1, x.shape[-1])
        h = jax.nn.silu(xf @ Wg) * (xf @ Wu)
        out = h @ Wd
        return out.reshape(x.shape[:-1] + (Wd.shape[1],))

    def _L1_attn_ref(data, mask, weight, bias):
        import jax, jax.numpy as jnp
        import numpy as np
        BH = 32
        BW = 32
        N, K = weight.shape
        Nb, Kb = (N // BH, K // BW)
        bm = mask.reshape(Nb, BH, Kb, BW).sum(axis=(1, 3)) > 0
        wb = weight.reshape(Nb, BH, Kb, BW) * bm[:, None, :, None].astype(weight.dtype)
        w = wb.reshape(N, K)
        out = jnp.einsum('bsk,nk->bsn', data, w) + bias
        return out

    def _L1_ffn_ref(x, W_base, b_base, enc0, enc1, coefs0, coefs1, mask0, mask1):
        import math
        import jax, jax.numpy as jnp
        import numpy as np
        SCALING = 16.0 / 32.0

        def real_fourier_orthogonal_multiply(c):
            n = c.shape[-1]
            sqrt_n = math.sqrt(n)
            pair_scale = math.sqrt(n / 2.0)
            max_f = (n - 1) // 2
            work = c.astype(jnp.float32)
            dc = (work[..., 0] * sqrt_n)[..., None].astype(jnp.complex64)
            cos = work[..., 1:1 + 2 * max_f:2] * pair_scale
            sin = work[..., 2:2 + 2 * max_f:2] * pair_scale
            mid = (cos - 1j * sin).astype(jnp.complex64)
            parts = [dc, mid]
            if n % 2 == 0:
                parts.append((work[..., -1] * sqrt_n)[..., None].astype(jnp.complex64))
            spectrum = jnp.concatenate(parts, axis=-1)
            return jnp.fft.irfft(spectrum, n=n, axis=-1).astype(c.dtype)
        base = jnp.einsum('bsd,od->bso', x, W_base) + b_base
        e0 = jnp.einsum('bsd,rd->bsr', x, enc0)
        e1 = jnp.einsum('bsd,rd->bsr', x, enc1)
        w0 = coefs0 * mask0.astype(coefs0.dtype)
        w1 = coefs1 * mask1.astype(coefs1.dtype)
        decoded = jnp.einsum('bsr,eor->ebso', e0, w0) + jnp.einsum('bsr,eor->ebso', e1, w1)
        transformed = real_fourier_orthogonal_multiply(decoded)
        update = transformed.sum(axis=0)
        return base + update * SCALING
    x = L0_attn_hidden_states
    x = x + _layernorm(_L0_attn_ref(_layernorm(x, axis=-1), L0_attn_Wqkv, L0_attn_Wo), axis=-1)
    x = x + _layernorm(_L0_ffn_ref(_layernorm(x, axis=-1), L0_ffn_gate_qweight, L0_ffn_gate_scales, L0_ffn_gate_qzeros, L0_ffn_gate_g_idx, L0_ffn_up_qweight, L0_ffn_up_scales, L0_ffn_up_qzeros, L0_ffn_up_g_idx, L0_ffn_down_qweight, L0_ffn_down_scales, L0_ffn_down_qzeros, L0_ffn_down_g_idx), axis=-1)
    x = x + _layernorm(_L1_attn_ref(_layernorm(x, axis=-1), L1_attn_mask, L1_attn_weight, L1_attn_bias), axis=-1)
    x = x + _layernorm(_L1_ffn_ref(_layernorm(x, axis=-1), L1_ffn_W_base, L1_ffn_b_base, L1_ffn_enc0, L1_ffn_enc1, L1_ffn_coefs0, L1_ffn_coefs1, L1_ffn_mask0, L1_ffn_mask1), axis=-1)
    return x

_drawn_inputs = setup_inputs


def setup_inputs(seed=0):
    import zlib

    import numpy as np

    out = dict(_drawn_inputs(seed))
    spreads = {}
    factors = {'L1_ffn_b_base': 3.226, 'L1_ffn_enc1': 4.166, 'L1_ffn_coefs1': 4.198}
    for name, (base, spread) in spreads.items():
        noise = np.random.default_rng([zlib.crc32(name.encode()), seed]).standard_normal(out[name].shape)
        drawn = base * np.exp(spread * noise) if base else spread * noise
        out[name] = jnp.asarray(drawn.astype(out[name].dtype))
    for name, factor in factors.items():
        out[name] = (out[name] * factor).astype(out[name].dtype)
    return out
```

```python
from contextlib import ExitStack

import concourse.bass as bass
from concourse import mybir

ALU = mybir.AluOpType
ACT = mybir.ActivationFunctionType
AX = mybir.AxisListType
F32 = mybir.dt.float32
F32R = mybir.dt.float32r
BF16 = mybir.dt.bfloat16
I32 = mybir.dt.int32
U8 = mybir.dt.uint8

P = 128
B, S, D = 2, 1024, 512
NH, HD = 32, 16
DC = D // P
QB = S // P
HALF = 512
EPS = 1e-5

QK_ROWS = 6 * HD
POS_ROWS = 9
P1_ROWS = QK_ROWS + POS_ROWS
P2_ROWS = P1_ROWS + 3
Q_PART = [0, 0, 0, 1, 1, 2]


def hi(ap):
    return ap.bitcast(F32R)


def three_pass(pe, out, w_hi, w_lo, x_hi, x_lo, chunks):
    for c in range(chunks):
        pe.matmul(out, w_hi(c), x_hi(c), start=(c == 0), stop=False)
        pe.matmul(out, w_hi(c), x_lo(c), start=False, stop=False)
        last = pe.matmul(out, w_lo(c), x_hi(c), start=False, stop=(c == chunks - 1))
    return last



def pass1_uses(qb):
    uses = [("diag", qb, h, 8) for h in range(0, NH, 8)]
    if qb:
        n = 2 * max(1, 512 // (qb * P)) if qb <= 4 else 1
        uses += [("off", qb, h, n) for h in range(0, NH, n)]
    return uses


def chunk_uses(hf):
    return [("xt", hf, t) for t in range(4)] + [("q", hf, 0), ("q", hf, 1)], [("kv", hf), ("vt", hf)]


def alternate(a, b):
    return [x for pair in zip(a, b) for x in pair] + a[len(b):] + b[len(a):]


LONG = (6, 7)
AHEAD = {1: 4, 4: 3, 5: 3, 6: 3, 7: 3}


def stage_events(s):
    queries, keys = chunk_uses(0 if s >= QB else 1)
    made = {2: queries, 3: keys, QB: queries, QB + 1: keys}.get(s, [])
    posts = [(k, s - 2) for k in ("ot", "at", "wo")] if 2 <= s else []
    if s == QB + 1:
        return [("use", u) for u in alternate(posts, made)]
    uses = alternate(pass1_uses(s), made) + [("mt", s)] if s < QB else made
    tiles = 8 * s if 1 <= s <= QB else 0
    if not tiles:
        return [("use", u) for u in uses]
    ahead = AHEAD.get(s, 2)
    events, done = [("use", u) for u in uses[:ahead]], ahead
    at = {max(1, tiles * (j + 1) // 5): u for j, u in enumerate(posts)}
    spread = tiles - (4 if s in LONG else 1)
    if s == QB:
        spread = tiles * 3 // 4
    for k in range(tiles):
        events.append(("tile", (s - 1, k)))
        if k in at:
            events.append(("use", at[k]))
        upto = min(len(uses), ahead - (-(len(uses) - ahead) * (k + 1) // spread))
        events += [("use", u) for u in uses[done:upto]]
        done = upto
    return events


FIRST_USES = {u: n for n, u in enumerate(chunk_uses(0)[0] + chunk_uses(0)[1])}
USES = [e[1] for s in range(QB + 2) for e in stage_events(s) if e[0] == "use"]
USES = {u: n for n, u in enumerate(USES)}
PER_BATCH = len(USES)
TILES = 4 * QB * (QB + 1)
assert PER_BATCH % 2 == 0 and len(FIRST_USES) % 2 == 0 and TILES % 4 == 0


def number(b, u):
    return FIRST_USES[u] if b is None else b * PER_BATCH + (len(FIRST_USES) + USES[u])


def chunk(b, hf):
    return 0 if b is None else b * 2 + (2 - hf)


def tile_no(qb, k):
    return 4 * qb * (qb + 1) + k


def attention(nc, x_dram, wqkv, wo, ident_d, identb_d, mask_d, qrows_d, krows_d, gmask_d, q_scratch, x1_dram, ident, identb, next_loads, next_in):
    with ExitStack() as ctx:
        def sb(name, shape, dt=F32):
            return ctx.enter_context(nc.sbuf_tensor(name, shape, dt))

        def sem(name):
            return ctx.enter_context(nc.semaphore(name))

        mask = sb("mask", [P, 2, 512], BF16)
        gmask = sb("gmask", [P, 3])
        half_neg = sb("half_neg", [P, 4])
        raw = sb("raw", [P, DC, D + 2 * HD])
        wo_raw = sb("wo_raw", [P, DC, D])
        wx = [sb(f"wx{i}", [P, DC, D + P]) for i in range(2)]
        wo_s = [sb(f"wo{i}", [P, DC, D]) for i in range(2)]
        xin = sb("xin", [P, 4, D])
        xT = [sb(f"xT{i}", [P, DC, HALF]) for i in range(2)]
        stats = sb("stats", [P, 4, 6])
        moments = sb("moments", [P, 4, 2])
        rstd = sb("rstd", [P, 4])
        kvf = sb("kvf", [P, HALF])
        kpart = [sb(f"kpart{i}", [P, HALF], BF16) for i in range(2)]
        krest = sb("krest", [P, HALF])
        KS = sb("KS", [P2_ROWS, S], BF16)
        V = sb("V", [P, QB, 32])
        QP = sb("QP", [P, 3, DC, HALF], BF16)
        qrest = sb("qrest", [P, 2, HALF])
        QS = [sb(f"QS{i}", [P2_ROWS, NH, HALF], BF16) for i in range(2)]
        mdiag = sb("mdiag", [P, 2, NH])
        moff = sb("moff", [P, 2, NH])
        nmax = sb("nmax", [P, 2, NH])
        mparts = sb("mparts", [NH, 2, 3, P], BF16)
        mrest = sb("mrest", [NH, 2, 2, P])
        PT = sb("PT", [P, 4, 512])
        OT = sb("OT", [P, 2, 512])
        rsum = sb("rsum", [P, 2, NH])
        A = sb("A", [P, D])
        aT = [sb(f"aT{i}", [P, DC, P]) for i in range(2)]
        ystats = sb("ystats", [P, 2, 6])
        ymom = sb("ymom", [P, 2, 2])
        yrstd = sb("yrstd", [P, 2])
        y = sb("y", [P, 2, D])
        xres = sb("xres", [P, 2, D])
        xout = sb("xout", [P, 2, D])

        pair = ctx.enter_context(nc.psum_tensor("pair", [P, 2, 2, 512], F32))
        ST = ctx.enter_context(nc.psum_tensor("ST", [P, 2, 512], F32))
        PO = ctx.enter_context(nc.psum_tensor("PO", [P, 2, 512], F32))

        consts_in = sem("consts_in")
        stack_in = sem("stack_in")
        w_in = sem("w_in")
        wo_in = sem("wo_in")
        wx_hi = sem("wx_hi")
        wx_lo = sem("wx_lo")
        wo_hi = sem("wo_hi")
        wo_lo = sem("wo_lo")
        init = sem("init")
        waited = sem("waited")
        x_in = sem("x_in")
        res_in = [sem(f"res_in{i}") for i in range(2)]
        pair_full = sem("pair_full")
        pair_free = sem("pair_free")
        dve = sem("dve")
        ln_var = sem("ln_var")
        ln_rstd = sem("ln_rstd")
        xn_ready = sem("xn_ready")
        xthi = sem("xthi")
        kv_ready = sem("kv_ready")
        ks_ready = sem("ks_ready")
        q1_ready = sem("q1_ready")
        qr_ready = sem("qr_ready")
        q2_ready = sem("q2_ready")
        q3_ready = sem("q3_ready")
        q_out = sem("q_out")
        qs_in = [[sem(f"qs_in{i}{g}") for g in range(2)] for i in range(2)]
        m_ready = sem("m_ready")
        nm_ready = sem("nm_ready")
        m_in = [sem(f"m_in{i}") for i in range(2)]
        st_full = sem("st_full")
        p_done = sem("p_done")
        pv_done = sem("pv_done")
        ot_done = sem("ot_done")
        a_ready = sem("a_ready")
        athi = sem("athi")
        y_var = sem("y_var")
        y_rstd = sem("y_rstd")
        y_ready = sem("y_ready")
        x1_ready = sem("x1_ready")
        x1_out = [sem(f"x1_out{i}") for i in range(2)]

        def pair_at(b, u):
            n = FIRST_USES[u] if b is None else len(FIRST_USES) + USES[u]
            return pair[:, n % 2, :, :]

        def full(eng, b, u):
            eng.wait_ge(pair_full, number(b, u) + 1)

        def released(eng, b, u):
            eng.wait_ge(pair_free, number(b, u) + 3)

        block = ctx.enter_context(nc.Block())

        @block.sync
        def _(sp):
            sp.dma_start(xin[:, :, :], x_dram[0:HALF, :].rearrange("(t p) d -> p t d", p=P)).then_inc(x_in, 16)
            for dst, src in ((ident, ident_d), (gmask, gmask_d)):
                sp.dma_start(dst[:], src).then_inc(consts_in, 16)
            sp.dma_start(raw[:, :, :], wqkv.rearrange("(c p) n -> p c n", p=P)).then_inc(w_in, 16)
            for dst, src in ((identb, identb_d), (mask, mask_d)):
                sp.dma_start(dst[:], src).then_inc(stack_in, 16)
            sp.dma_start(KS[QK_ROWS:P2_ROWS, :], krows_d).then_inc(stack_in, 16)
            for hf in range(2):
                sp.dma_start(QS[hf][QK_ROWS:P1_ROWS, :, :], qrows_d[:, :, hf * HALF:(hf + 1) * HALF]).then_inc(stack_in, 16)
            sp.dma_start(wo_raw[:, :, :], wo.rearrange("(c p) n -> p c n", p=P)).then_inc(wo_in, 16)
            for i in range(2):
                sp.sem_inc(x1_out[i], 16)
                sp.sem_inc(m_in[i], 48)

            def stack_q(b, hf):
                n = chunk(b, hf)
                for g in range(2):
                    for part, ready in enumerate((q1_ready, q2_ready, q3_ready)):
                        sp.wait_ge(ready, n * 4 + (2 * g + 2))
                        sp.dma_start(q_scratch[part, 2 * g:2 * g + 2].rearrange("m h d q -> (h d) m q"),
                                     QP[:, part, 2 * g:2 * g + 2, :]).then_inc(q_out, 16)
                    sp.wait_ge(q_out, n * 96 + (g + 1) * 48)
                    for row, part in enumerate(Q_PART):
                        sp.dma_start(QS[hf][row * HD:(row + 1) * HD, 16 * g:16 * (g + 1), :],
                                     q_scratch[part, 2 * g:2 * g + 2].rearrange("m h d q -> d (m h) q")).then_inc(qs_in[hf][g], 16)

            stack_q(None, 0)
            for dst, src in next_loads:
                sp.dma_start(dst, src, allow_slow_non_contiguous=True).then_inc(next_in, 16)
            with sp.Fori(0, B) as b:
                second_half = sp.snap(b * S + HALF)
                tok = [sp.snap(b * S + q * P) for q in range(QB)]

                def load_x(row, turned):
                    sp.wait_ge(xthi, turned)
                    sp.dma_start(xin[:, :, :], x_dram[bass.ds(row, HALF), :].rearrange("(t p) d -> p t d", p=P)).then_inc(x_in, 16)

                def stack_max(qb):
                    sp.wait_ge(m_ready, b * QB + qb + 1)
                    hf, i = divmod(qb, 4)
                    for j in range(3):
                        sp.dma_start(QS[hf][P1_ROWS + j:P1_ROWS + j + 1, :, i * P:(i + 1) * P],
                                     mparts[:, qb % 2, j, :]).then_inc(m_in[qb % 2], 16)

                def load_res(qb):
                    sp.wait_ge(x1_ready, b * QB + qb + 1)
                    sp.dma_start(xres[:, qb % 2, :], x_dram[bass.ds(tok[qb], P), :]).then_inc(res_in[qb % 2], 16)

                def store_x1(qb):
                    sp.wait_ge(x1_ready, b * QB + qb + 3)
                    sp.dma_start(x1_dram[bass.ds(tok[qb], P), :], xout[:, qb % 2, :]).then_inc(x1_out[qb % 2], 16)

                load_x(second_half, b * 8 + 4)
                for s in range(QB + 2):
                    if s < QB:
                        if s < 2:
                            load_res(s)
                        if s == 2:
                            stack_q(b, 1)
                        if s == 3:
                            load_x(S, b * 8 + 8)
                        stack_max(s)
                    if s == QB:
                        stack_q(b, 0)
                    if s >= 2:
                        store_x1(s - 2)
                        if s < QB:
                            load_res(s)
            for i in range(2):
                sp.wait_ge(x1_out[i], 16 * B * QB // 2 + 16)
                sp.wait_ge(qs_in[0][i], 96 * (B + 1))
            sp.wait_ge(next_in, 16 * len(next_loads))

        @block.gpsimd
        def _(pool):
            pool.memset(half_neg[:, :], -0.5).then_inc(init, 1)
            pool.sem_inc(x1_ready, 2)
            pool.wait_ge(init, 1)

            def chunk_rstd(b, hf):
                pool.wait_ge(ln_var, chunk(b, hf) + 1)
                pool.tensor_tensor(rstd[:, :], moments[:, :, 1], half_neg[:, :], ALU.pow).then_inc(ln_rstd, 1)

            def q_third(b, hf, m):
                pool.wait_ge(q2_ready, chunk(b, hf) * 4 + (m + 1))
                pool.tensor_tensor(QP[:, 2, m, :], qrest[:, m % 2, :], QP[:, 1, m, :], ALU.subtract).then_inc(q3_ready, 1)

            chunk_rstd(None, 0)
            for m in range(4):
                q_third(None, 0, m)
            pool.wait_ge(wo_hi, 1)
            pool.tensor_tensor(hi(wo_s[1][:, :, :]), wo_raw[:, :, :], wo_s[0][:, :, :], ALU.subtract).then_inc(wo_lo, 1)
            with pool.Fori(0, B) as b:
                for s in range(QB + 2):
                    if s in (2, QB):
                        chunk_rstd(b, int(s == 2))
                    for kind, e in stage_events(s):
                        if kind == "use" and e[0] == "q":
                            q_third(b, e[1], 2 * e[2])
                            q_third(b, e[1], 2 * e[2] + 1)
                        if kind == "use" and e[0] == "wo":
                            qb = e[1]
                            pool.wait_ge(y_var, b * QB + qb + 1)
                            pool.tensor_tensor(yrstd[:, qb % 2:qb % 2 + 1], ymom[:, qb % 2, 1:2], half_neg[:, 0:1], ALU.pow).then_inc(y_rstd, 1)
                            pool.wait_ge(y_rstd, b * QB + qb + 1)
                            released(pool, b, e)
                            pool.sem_inc(waited, 1)
                            pool.tensor_scalar(y[:, qb % 2, :], y[:, qb % 2, :], ymom[:, qb % 2, 0:1], yrstd[:, qb % 2:qb % 2 + 1],
                                               ALU.subtract, ALU.mult).then_inc(y_ready, 1)
                            pool.wait_ge(y_ready, b * QB + qb + 1)
                            pool.wait_ge(res_in[qb % 2], (b * QB // 2 + qb // 2 + 1) * 16)
                            pool.wait_ge(x1_out[qb % 2], (b * QB // 2 + qb // 2 + 1) * 16)
                            pool.tensor_tensor(xout[:, qb % 2, :], y[:, qb % 2, :], xres[:, qb % 2, :], ALU.add).then_inc(x1_ready, 1)

        @block.scalar
        def _(act):
            act.sem_inc(p_done, 2)
            act.sem_inc(ot_done, 2)
            act.wait_ge(w_in, 16)
            act.activation(hi(wx[0][:, :, 0:D]), raw[:, :, 0:D], ACT.Copy).then_inc(wx_hi, 1)
            for g in range(8):
                src = raw[:, :, D:D + HD] if g < 6 else raw[:, :, D + HD:D + 2 * HD]
                act.activation(hi(wx[0][:, :, D + g * HD:D + (g + 1) * HD]), src, ACT.Copy).then_inc(wx_hi, 1)

            def xt_hi(b, hf, t):
                full(act, b, ("xt", hf, t))
                act.activation(hi(xT[0][:, :, t * P:(t + 1) * P]),
                               pair_at(b, ("xt", hf, t))[:, 0, :].rearrange("p (c q) -> p c q", c=DC), ACT.Copy).then_inc(xthi, 1)

            def q_parts(b, hf, g):
                full(act, b, ("q", hf, g))
                for mm in range(2):
                    act.activation(QP[:, 0, 2 * g + mm, :], pair_at(b, ("q", hf, g))[:, mm, :], ACT.Copy, scale=HD ** -0.5).then_inc(q1_ready, 1)
                for mm in range(2):
                    act.wait_ge(qr_ready, chunk(b, hf) * 4 + (2 * g + mm + 1))
                    act.activation(QP[:, 1, 2 * g + mm, :], qrest[:, mm, :], ACT.Copy).then_inc(q2_ready, 1)

            for t in range(4):
                xt_hi(None, 0, t)
            for g in range(2):
                q_parts(None, 0, g)
            act.wait_ge(wo_in, 16)
            act.activation(hi(wo_s[0][:, :, :]), wo_raw[:, :, :], ACT.Copy).then_inc(wo_hi, 1)
            with act.Fori(0, B) as b:
                for s in range(QB + 2):
                    if s >= 2:
                        qb = s - 2
                        act.wait_ge(pv_done, b * TILES + tile_no(qb + 1, 0) + 4)
                        for k in range(2):
                            act.activation(OT[:, k, :], PO[:, k, :], ACT.Copy).then_inc(ot_done, 1)
                    for kind, e in stage_events(s):
                        if kind == "tile":
                            n = tile_no(*e)
                            act.wait_ge(st_full, b * TILES + n + 1)
                            act.wait_ge(pv_done, b * TILES + n + 1)
                            act.activation(PT[:, n % 4, :], ST[:, n % 2, :], ACT.Exp).then_inc(p_done, 1)
                        elif e[0] == "xt":
                            xt_hi(b, *e[1:])
                        elif e[0] == "q":
                            q_parts(b, *e[1:])
                        elif e[0] == "at":
                            full(act, b, e)
                            act.activation(hi(aT[0][:, :, :]), pair_at(b, e)[:, 0, :].rearrange("p (c q) -> p c q", c=DC), ACT.Copy).then_inc(athi, 1)

        @block.vector
        def _(v):
            chain = [0]
            v.sem_inc(pair_free, 2)
            v.memset(V[:, :, 0:HD], 0.0).then_inc(dve, 1)
            v.memset(V[:, :, HD:HD + 1], 1.0).then_inc(dve, 1)
            v.memset(V[:, :, HD + 1:32], 0.0).then_inc(dve, 1)
            v.wait_ge(dve, 3)
            v.memset(moff[:, :, :], 0.0).then_inc(dve, 1)
            PER = 2 * (8 + 3) + QB * (3 + 1 + 2) + QB - 1

            FIRST = 4 + 8 + 3

            def linked(b):
                return chain[0] + (0 if b is None else b * PER)

            def link(b, ins):
                chain[0] += 1
                ins.then_inc(dve, 1)
                v.wait_ge(dve, linked(b))

            def tick(ins):
                chain[0] += 1
                ins.then_inc(dve, 1)

            def norm_chunk(b, hf):
                v.wait_ge(x_in, chunk(b, hf) * 16 + 16)
                for t in range(4):
                    tick(v.bn_stats(stats[:, t, :], xin[:, t, :]))
                v.wait_ge(dve, linked(b))
                v.sem_inc(waited, 1)
                for t in range(4):
                    tick(v.bn_aggr(moments[:, t, :], stats[:, t, :]))
                v.wait_ge(dve, linked(b))
                v.tensor_scalar(moments[:, :, 1], moments[:, :, 1], EPS, None, ALU.add).then_inc(ln_var, 1)
                v.wait_ge(ln_rstd, chunk(b, hf) + 1)
                for t in range(4):
                    v.tensor_scalar(xin[:, t, :], xin[:, t, :], moments[:, t, 0:1], rstd[:, t:t + 1], ALU.subtract, ALU.mult).then_inc(xn_ready, 1)

            def max_rest(b, qb):
                u = ("mt", qb)
                full(v, b, u)
                v.wait_ge(m_in[qb % 2], (b * QB // 2 + qb // 2 + 1) * 48)
                src = pair_at(b, u)[0:NH, 0, 0:P]
                k = qb % 2
                link(b, v.tensor_copy(mparts[:, k, 0, :], src))
                v.tensor_tensor(mrest[:, k, 0, :], src, mparts[:, k, 0, :], ALU.subtract).then_inc(pair_free, 1)
                released(v, b, u)
                link(b, v.tensor_copy(mparts[:, k, 1, :], mrest[:, k, 0, :]))
                link(b, v.tensor_tensor(mrest[:, k, 1, :], mrest[:, k, 0, :], mparts[:, k, 1, :], ALU.subtract))
                v.tensor_copy(mparts[:, k, 2, :], mrest[:, k, 1, :]).then_inc(m_ready, 1)

            def use(b, u):
                kind, src = u[0], pair_at(b, u)
                if kind == "mt":
                    return max_rest(b, u[1])
                full(v, b, u)
                if kind == "xt":
                    _, hf, t = u
                    v.wait_ge(xthi, chunk(b, hf) * 4 + (t + 1))
                    at = slice(t * P, (t + 1) * P)
                    v.tensor_tensor(hi(xT[1][:, :, at]), src[:, 0, :].rearrange("p (c q) -> p c q", c=DC), xT[0][:, :, at],
                                    ALU.subtract).then_inc(pair_free, 1)
                elif kind == "kv":
                    hf = u[1]
                    v.tensor_copy(kvf[:, :], src[:, 0, :]).then_inc(pair_free, 1)
                    released(v, b, u)
                    k = slice(0, QK_ROWS)
                    link(b, v.tensor_copy(kpart[0][k, :], kvf[k, :]))
                    link(b, v.scalar_tensor_tensor(krest[k, :], kpart[0][k, :], gmask[k, 0:1], kvf[k, :], ALU.mult, ALU.add))
                    link(b, v.tensor_copy(kpart[1][k, :], krest[k, :]))
                    v.scalar_tensor_tensor(KS[k, hf * HALF:(hf + 1) * HALF], kpart[1][k, :], gmask[k, 1:2], krest[k, :],
                                           ALU.mult, ALU.add).then_inc(ks_ready, 1)
                elif kind == "vt":
                    hf = u[1]
                    v.tensor_copy(V[:, 4 * hf:4 * hf + 4, 0:HD],
                                  src[:, 0, :].rearrange("p (t r) -> p t r", t=4)[:, :, QK_ROWS:QK_ROWS + HD]).then_inc(pair_free, 1)
                elif kind == "q":
                    _, hf, g = u
                    for mm in range(2):
                        n = chunk(b, hf) * 4 + (2 * g + mm)
                        v.wait_ge(q1_ready, n + 1)
                        if g:
                            v.wait_ge(q3_ready, n - 1)
                        v.scalar_tensor_tensor(qrest[:, mm, :], src[:, mm, :], HD ** -0.5, QP[:, 0, 2 * g + mm, :],
                                               ALU.mult, ALU.subtract).then_inc(qr_ready, 1)
                    v.wait_ge(qr_ready, chunk(b, hf) * 4 + (2 * g + 2))
                    v.sem_inc(pair_free, 1)
                elif kind == "diag":
                    _, qb, h, n = u
                    v.tensor_reduce(mdiag[:, qb % 2, h:h + n], src.rearrange("p a (h k) -> p (a h) k", k=P), AX.X, ALU.max).then_inc(pair_free, 1)
                elif kind == "off":
                    _, qb, h, n = u
                    w = qb * P
                    if n == 1:
                        v.tensor_reduce(moff[:, qb % 2, h:h + 1], src.rearrange("p a k -> p (a k)")[:, 0:w], AX.X, ALU.max).then_inc(pair_free, 1)
                    else:
                        m = n // 2
                        view = src[:, :, 0:m * w].rearrange("p a (m k) -> p a m k", k=w)
                        v.tensor_reduce(moff[:, qb % 2, h:h + n], view if m > 1 else src[:, :, 0:w], AX.X, ALU.max).then_inc(pair_free, 1)
                elif kind == "ot":
                    qb = u[1]
                    flat = src.rearrange("p a (s c) -> p (a s) c", c=32)
                    link(b, v.reciprocal(rsum[:, qb % 2, :], flat[:, :, HD]))
                    for a in range(2):
                        ins = v.tensor_tensor(
                            A[:, a * 256:(a + 1) * 256].rearrange("p (j i d) -> p i j d", j=4, i=4),
                            src[:, a, :].rearrange("p (i j c) -> p i j c", j=4, c=32)[:, :, :, 0:HD],
                            rsum[:, qb % 2, a * 16:(a + 1) * 16].rearrange("p (i j) -> p i j", j=4).unsqueeze(3).to_broadcast([P, 4, 4, HD]),
                            ALU.mult)
                        ins.then_inc(a_ready, 1) if a == 0 else ins.then_inc(pair_free, 1)
                elif kind == "at":
                    v.wait_ge(athi, b * QB + u[1] + 1)
                    v.tensor_tensor(hi(aT[1][:, :, :]), src[:, 0, :].rearrange("p (c q) -> p c q", c=DC), aT[0][:, :, :],
                                    ALU.subtract).then_inc(pair_free, 1)
                elif kind == "wo":
                    k = u[1] % 2
                    v.wait_ge(x1_ready, b * QB + u[1] + 1)
                    tick(v.bn_stats(ystats[:, k, :], src[:, 0, :]))
                    v.tensor_copy(y[:, k, :], src[:, 0, :]).then_inc(pair_free, 1)
                    v.wait_ge(dve, linked(b))
                    v.sem_inc(waited, 1)
                    link(b, v.bn_aggr(ymom[:, k, :], ystats[:, k, :]))
                    v.tensor_scalar(ymom[:, k, 1:2], ymom[:, k, 1:2], EPS, None, ALU.add).then_inc(y_var, 1)
                last = [w for w in pass1_uses(u[1])][-1] if kind in ("diag", "off") else None
                if u == last:
                    qb = u[1]
                    k = qb % 2
                    released(v, b, u)
                    if qb:
                        link(b, v.tensor_tensor(mdiag[:, k, :], mdiag[:, k, :], moff[:, k, :], ALU.max))
                    v.tensor_scalar(nmax[:, k, :], mdiag[:, k, :], -1.0, None, ALU.mult).then_inc(nm_ready, 1)

            chain[0] = 4
            norm_chunk(None, 0)
            v.wait_ge(w_in, 16)
            for g in range(9):
                src = raw[:, :, 0:D] if g == 0 else raw[:, :, D:D + HD] if g < 7 else raw[:, :, D + HD:D + 2 * HD]
                at = slice(0, D) if g == 0 else slice(D + (g - 1) * HD, D + g * HD)
                v.wait_ge(wx_hi, g + 1)
                v.tensor_tensor(hi(wx[1][:, :, at]), src, wx[0][:, :, at], ALU.subtract).then_inc(wx_lo, 1)
            v.wait_ge(consts_in, 32)
            for u in FIRST_USES:
                use(None, u)
            assert chain[0] == FIRST
            with v.Fori(0, B) as b:
                chain[0] = FIRST
                for s in range(QB + 2):
                    if s in (2, QB):
                        norm_chunk(b, int(s == 2))
                    for kind, e in stage_events(s):
                        if kind == "use":
                            use(b, e)
                assert chain[0] == FIRST + PER

        @block.tensor
        def _(pe):
            pe.sem_inc(pv_done, 4)
            pe.wait_ge(consts_in, 32)

            def use(b, u):
                kind, dst = u[0], pair_at(b, u)
                pe.wait_ge(pair_free, number(b, u) + 1)
                if kind == "xt":
                    _, hf, t = u
                    pe.wait_ge(xn_ready, chunk(b, hf) * 4 + (t + 1))
                    for c in range(DC):
                        last = pe.transpose(dst[:, 0, c * P:(c + 1) * P], xin[:, t, c * P:(c + 1) * P], ident[:, :])
                elif kind == "kv":
                    released(pe, b, ("xt", u[1], 3))
                    last = three_pass(pe, dst[:, 0, :], lambda c: hi(wx[0][:, c, D:D + P]), lambda c: hi(wx[1][:, c, D:D + P]),
                                      lambda c: hi(xT[0][:, c, :]), lambda c: hi(xT[1][:, c, :]), DC)
                elif kind == "vt":
                    released(pe, b, ("kv", u[1]))
                    for t in range(4):
                        last = pe.transpose(dst[:, 0, t * P:(t + 1) * P], kvf[:, t * P:(t + 1) * P], ident[:, :])
                elif kind == "q":
                    pe.wait_ge(wx_lo, 9)
                    released(pe, b, ("xt", u[1], 3))
                    for mm in range(2):
                        at = slice((2 * u[2] + mm) * P, (2 * u[2] + mm + 1) * P)
                        last = three_pass(pe, dst[:, mm, :], lambda c: hi(wx[0][:, c, at]), lambda c: hi(wx[1][:, c, at]),
                                          lambda c: hi(xT[0][:, c, :]), lambda c: hi(xT[1][:, c, :]), DC)
                elif kind == "diag":
                    _, qb, h0, n = u
                    hf, i = divmod(qb, 4)
                    for g in range(h0 // 16, 1 + (h0 + n - 1) // 16):
                        pe.wait_ge(qs_in[hf][g], (b + 1) * 96)
                    pe.wait_ge(ks_ready, b * 2 + (hf + 1))
                    for a in range(2):
                        for j in range(4):
                            pe.matmul(dst[:, a, j * P:(j + 1) * P], QS[hf][0:P1_ROWS, h0 + 4 * a + j, i * P:(i + 1) * P],
                                      KS[0:P1_ROWS, qb * P:(qb + 1) * P], start=(j == 0), stop=False, skip_group_check=True)
                        last = pe.matmul(dst[:, a, :], identb[:, :], mask[:, 0, :], start=False, stop=True, skip_group_check=True)
                elif kind == "off":
                    _, qb, h0, n = u
                    hf, i = divmod(qb, 4)
                    w = qb * P
                    for j in range(n):
                        q = QS[hf][0:P1_ROWS, h0 + j, i * P:(i + 1) * P]
                        if n == 1:
                            flat = dst.rearrange("p a k -> p (a k)")
                            for k in range(0, w, 512):
                                last = pe.matmul(flat[:, k:min(w, k + 512)], q, KS[0:P1_ROWS, k:min(w, k + 512)], start=True, stop=True)
                        else:
                            a, m = divmod(j, n // 2)
                            last = pe.matmul(dst[:, a, m * w:(m + 1) * w], q, KS[0:P1_ROWS, 0:w], start=True, stop=True)
                elif kind == "mt":
                    pe.wait_ge(nm_ready, b * QB + u[1] + 1)
                    last = pe.transpose(dst[0:NH, 0, 0:P], nmax[:, u[1] % 2, :], ident[:, :])
                elif kind == "ot":
                    pe.wait_ge(ot_done, (b * QB + u[1]) * 2 + 4)
                    for a in range(2):
                        for i in range(4):
                            last = pe.transpose(dst[:, a, i * P:(i + 1) * P], OT[:, a, i * P:(i + 1) * P], ident[:, :])
                elif kind == "at":
                    released(pe, b, ("ot", u[1]))
                    for c in range(DC):
                        last = pe.transpose(dst[:, 0, c * P:(c + 1) * P], A[:, c * P:(c + 1) * P], ident[:, :])
                elif kind == "wo":
                    released(pe, b, ("at", u[1]))
                    last = three_pass(pe, dst[:, 0, :], lambda c: hi(aT[0][:, c, :]), lambda c: hi(aT[1][:, c, :]),
                                      lambda c: hi(wo_s[0][:, c, :]), lambda c: hi(wo_s[1][:, c, :]), DC)
                last.then_inc(pair_full, 1)

            for u in FIRST_USES:
                use(None, u)
            pe.wait_ge(stack_in, 16 * 5)
            pe.wait_ge(wo_lo, 1)
            with pe.Fori(0, B) as b:
                def scores(qb, k):
                    n = tile_no(qb, k)
                    kb, t = divmod(k, 8)
                    hf, i = divmod(qb, 4)
                    if k == 0:
                        pe.wait_ge(m_in[qb % 2], (b * QB // 2 + qb // 2 + 2) * 48)
                    pe.wait_ge(p_done, b * TILES + n + 1)
                    last = pe.matmul(ST[:, n % 2, :], KS[0:P2_ROWS, kb * P:(kb + 1) * P], QS[hf][0:P2_ROWS, 4 * t:4 * t + 4, i * P:(i + 1) * P],
                                     start=True, stop=(kb < qb))
                    if kb == qb:
                        last = pe.matmul(ST[:, n % 2, :], identb[:, :], mask[:, 1, :], start=False, stop=True)
                    last.then_inc(st_full, 1)

                def values(qb, k):
                    n = tile_no(qb, k)
                    kb, t = divmod(k, 8)
                    if k == 0:
                        pe.wait_ge(ot_done, (b * QB + qb) * 2 + 2)
                    pe.wait_ge(p_done, b * TILES + n + 3)
                    j = t % 4
                    pe.matmul(PO[32 * j:32 * (j + 1), t // 4, :], V[:, kb, :], PT[:, n % 4, :],
                              start=(kb == 0), stop=(kb == qb)).then_inc(pv_done, 1)

                LAG = 2
                for s in range(QB + 2):
                    before = 8 * (s - 1)
                    if s == QB + 1:
                        for k in range(before - LAG, before):
                            values(s - 2, k)
                    for kind, e in stage_events(s):
                        if kind == "use":
                            use(b, e)
                            continue
                        qb, k = e
                        if k == 0 and s >= 2:
                            for last in range(before - LAG, before):
                                values(qb - 1, last)
                        scores(qb, k)
                        if k >= LAG:
                            values(qb, k - LAG)



INTER = 1376
NT = -(-INTER // P)
PACK, BITS = 8, 4
GK, GD = 4, 10


def tile_w(n):
    return min(P, INTER - n * P)


GROUPS_OF = [GK, GK, GD]
FIRST_GROUP = [0, GK, 2 * GK]
G_ROWS = 2 * GK + GD
DQ_COL = [0, DC, 2 * DC]
DQ_COLS = 2 * DC + NT
DQ_UNITS = ([(m, [c], P, INTER) for c in range(DC) for m in range(2)]
            + [(2, list(range(n, min(n + 2, NT - 1))), P, D) for n in range(0, NT - 1, 2)] + [(2, [NT - 1], tile_w(NT - 1), D)])


def group_index_loads(mats, gidx):
    loads = []
    for m in range(3):
        whole = (INTER if m == 2 else D) // P
        loads.append((gidx[:, DQ_COL[m]:DQ_COL[m] + whole], mats[m][3][0:whole * P].rearrange("(c p) -> p c", p=P)))
    loads.append((gidx[0:tile_w(NT - 1), DQ_COLS - 1:DQ_COLS], mats[2][3][(NT - 1) * P:INTER].rearrange("(p c) -> p c", c=1)))
    return loads


def dequantize(nc, mats, ident, identb, shifts, group_ids, gidx, spare, gu, wd, next_loads, next_in):
    with ExitStack() as ctx:
        def sb(name, shape, dt=F32):
            return ctx.enter_context(nc.sbuf_tensor(name, shape, dt))

        def sem(name):
            return ctx.enter_context(nc.semaphore(name))

        W = INTER
        QW_RING, W_RING, BANKS = 2, 3, 4
        ztab = sb("d_ztab", [G_ROWS, W])
        s_raw = sb("d_s_raw", [2 * G_ROWS, W])
        stab = sb("d_stab", [2 * G_ROWS, W])
        gf = sb("d_gf", [P, DQ_COLS])
        gneg = sb("d_gneg", [P, DQ_COLS])
        onehot = sb("d_onehot", [P, DQ_COLS, 2 * G_ROWS])
        onehotT = sb("d_onehotT", [2 * G_ROWS, DQ_COLS, P])
        spare = [a[:].rearrange("p c n -> p (c n)") for a in spare]
        spare[1] = spare[1].bitcast(I32)
        qw = [spare[0][:, 0:W], spare[1][:, 0:W]]
        zpacked = spare[0][0:G_ROWS, W:W + W // PACK]
        q4 = sb("d_q4", [P, 2, W], BF16)
        wf = sb("d_wf", [P, W_RING, W])
        z4 = wf[0:G_ROWS, 1, :].bitcast(I32)
        s_hi = wf[0:2 * G_ROWS, 2, :]

        psum = ctx.enter_context(nc.psum_tensor("d_psum", [P, 2, BANKS, 512], F32))
        turn = psum[0:2 * G_ROWS].rearrange("p a b k -> p (a b) k")

        cleared = sem("d_cleared")
        z_in = sem("d_z_in")
        s_in = sem("d_s_in")
        chain = sem("d_chain")
        onehot_done = sem("d_onehot_done")
        turned = sem("d_turned")
        onehotT_done = sem("d_onehotT_done")
        s_hi_done = sem("d_s_hi_done")
        tables_done = sem("d_tables_done")
        qw_in = [sem(f"d_qw_in{i}") for i in range(QW_RING)]
        codes_done = sem("d_codes_done")
        picked = sem("d_picked")
        q4_done = sem("d_q4_done")
        wf_done = sem("d_wf_done")
        mul_done = sem("d_mul_done")
        hi_done = sem("d_hi_done")
        lo_done = sem("d_lo_done")

        units = DQ_UNITS
        pieces = [(u, c, i * w + a, a, min(512, w - a)) for u, (m, cs, r, w) in enumerate(units) for i, c in enumerate(cs)
                  for a in range(0, w, 512)]
        pieces_of = [[j for j, p in enumerate(pieces) if p[0] == u] for u in range(len(units))]

        def parts(u, i):
            m, cs, r, w = units[u]
            if m == 2:
                return wd[i][0:r, cs[0]:cs[-1] + 1, :].rearrange("p c n -> p (c n)")
            return gu[i][:, m, cs[0], :]

        def size(u):
            m, cs, r, w = units[u]
            return r, len(cs) * w

        block = ctx.enter_context(nc.Block())

        @block.sync
        def _(sp):
            def load_codes(u):
                m, cs, r, w = units[u]
                for i, c in enumerate(cs):
                    src = mats[m][0][c * P // PACK:(c * P + r) // PACK, :]
                    sp.dma_start(qw[u % QW_RING][0:r, i * w:(i + 1) * w],
                                 src.unsqueeze(1).to_broadcast([r // PACK, PACK, w])).then_inc(qw_in[u % QW_RING], 16)

            load_codes(0)
            for dst, src in next_loads:
                sp.dma_start(dst, src).then_inc(next_in, 16)
            sp.wait_ge(cleared, 2)
            for m in range(3):
                g0, g, w = FIRST_GROUP[m], GROUPS_OF[m], D if m == 2 else W
                sp.dma_start(zpacked[g0:g0 + g, 0:w // PACK], mats[m][2]).then_inc(z_in, 16)
                for i in range(2):
                    sp.dma_start(s_raw[i * G_ROWS + g0:i * G_ROWS + g0 + g, 0:w], mats[m][1]).then_inc(s_in, 16)
            for u in range(1, len(units)):
                if u >= QW_RING:
                    sp.wait_ge(q4_done, u - QW_RING + 1)
                load_codes(u)

        @block.gpsimd
        def _(pool):
            pool.memset(zpacked[:, :], 0).then_inc(cleared, 1)
            pool.memset(s_raw[:, :], 0.0).then_inc(cleared, 1)
            for u in range(len(units)):
                r, w = size(u)
                pool.wait_ge(hi_done, u + 1)
                pool.tensor_tensor(hi(parts(u, 1)), wf[0:r, u % W_RING, 0:w], parts(u, 0), ALU.subtract).then_inc(lo_done, 1)
            pool.wait_ge(lo_done, len(units))

        @block.vector
        def _(v):
            n_chain = [0]

            def link(ins):
                n_chain[0] += 1
                ins.then_inc(chain, 1)
                v.wait_ge(chain, n_chain[0])

            link(v.memset(gf[:, :], 0.0))
            link(v.tensor_copy(gf[:, 0:DQ_COLS - 1], gidx[:, 0:DQ_COLS - 1]))
            link(v.tensor_copy(gf[0:tile_w(NT - 1), DQ_COLS - 1:DQ_COLS], gidx[0:tile_w(NT - 1), DQ_COLS - 1:DQ_COLS]))
            for m in range(3):
                at = slice(DQ_COL[m], DQ_COL[m] + (NT if m == 2 else DC))
                link(v.tensor_scalar(gneg[:, at], gf[:, at], 0.0, float(GROUPS_OF[m]), ALU.is_lt, ALU.mult))
                link(v.tensor_tensor(gf[:, at], gf[:, at], gneg[:, at], ALU.add))
                link(v.tensor_scalar(gf[:, at], gf[:, at], 0.0, float(GROUPS_OF[m] - 1), ALU.max, ALU.min))
                link(v.tensor_scalar(gf[:, at], gf[:, at], float(FIRST_GROUP[m]), None, ALU.add))
            v.tensor_tensor(onehot[:], gf[:, :].unsqueeze(2).to_broadcast([P, DQ_COLS, 2 * G_ROWS]),
                            group_ids[:, 0:2 * G_ROWS].unsqueeze(1).to_broadcast([P, DQ_COLS, 2 * G_ROWS]), ALU.is_equal).then_inc(onehot_done, 1)

            def codes(u):
                r, w = size(u)
                v.wait_ge(qw_in[u % QW_RING], 16 * sum(len(units[x][1]) for x in range(u % QW_RING, u + 1, QW_RING)))
                at = qw[u % QW_RING][0:r, 0:w]
                v.tensor_scalar(at, at, shifts[0:r, 0:1], 15, ALU.logical_shift_right, ALU.bitwise_and).then_inc(codes_done, 1)
                if u >= 2:
                    v.wait_ge(picked, pieces_of[u - 2][-1] + 1)
                v.wait_ge(codes_done, u + 1)
                v.tensor_copy(q4[0:r, u % 2, 0:w], at).then_inc(q4_done, 1)

            codes(0)
            v.wait_ge(z_in, 16 * 3)
            for j in range(PACK):
                v.tensor_scalar(z4.rearrange("g (w j) -> g w j", j=PACK)[:, :, j], zpacked[:, :], BITS * j, 15, ALU.logical_shift_right,
                                ALU.bitwise_and).then_inc(chain, 1)
            n_chain[0] += PACK
            v.wait_ge(chain, n_chain[0])
            v.tensor_scalar(hi(ztab[:, :]), z4, -1.0, -1.0, ALU.mult, ALU.add).then_inc(tables_done, 1)
            v.wait_ge(s_hi_done, 1)
            v.scalar_tensor_tensor(hi(stab[:, :]), s_hi, group_ids[0:2 * G_ROWS, 2 * G_ROWS:2 * G_ROWS + 1], s_raw[:, :], ALU.mult, ALU.add).then_inc(tables_done, 1)
            v.wait_ge(tables_done, 2)

            for u in range(1, len(units) + 1):
                if u < len(units):
                    codes(u)
                r, w = size(u - 1)
                for j in pieces_of[u - 1]:
                    _, _, at, _, n = pieces[j]
                    v.wait_ge(wf_done, j + 1)
                    v.tensor_tensor(wf[0:r, (u - 1) % W_RING, at:at + n], wf[0:r, (u - 1) % W_RING, at:at + n], psum[0:r, 1, j % BANKS, 0:n],
                                    ALU.mult).then_inc(mul_done, 1)

        @block.scalar
        def _(act):
            act.wait_ge(s_in, 16 * 6)
            act.activation(hi(s_hi), s_raw[:, :], ACT.Copy).then_inc(s_hi_done, 1)
            for a in range(0, DQ_COLS, 4):
                n = min(4, DQ_COLS - a)
                act.wait_ge(turned, a + n)
                act.activation(hi(onehotT[:, a:a + n, :]), turn[:, a // 4, 0:n * P].rearrange("p (u k) -> p u k", k=P), ACT.Copy).then_inc(onehotT_done, 1)
            for u in range(len(units) + 1):
                if u < len(units):
                    r, w = size(u)
                    if u >= W_RING:
                        act.wait_ge(lo_done, u - W_RING + 1)
                    for j in pieces_of[u]:
                        _, _, at, _, n = pieces[j]
                        act.wait_ge(picked, j + 1)
                        act.activation(wf[0:r, u % W_RING, at:at + n], psum[0:r, 0, j % BANKS, 0:n], ACT.Copy).then_inc(wf_done, 1)
                if u:
                    r, w = size(u - 1)
                    act.wait_ge(mul_done, pieces_of[u - 1][-1] + 1)
                    act.activation(hi(parts(u - 1, 0)), wf[0:r, (u - 1) % W_RING, 0:w], ACT.Copy).then_inc(hi_done, 1)

        @block.tensor
        def _(pe):
            pe.wait_ge(onehot_done, 1)
            for a in range(DQ_COLS):
                pe.transpose(turn[:, a // 4, a % 4 * P:(a % 4 + 1) * P], onehot[:, a, :], ident[:, :]).then_inc(turned, 1)
            pe.wait_ge(onehotT_done, -(-DQ_COLS // 4))
            pe.wait_ge(tables_done, 2)
            for j, (u, c, at, a, n) in enumerate(pieces):
                m, r = units[u][0], units[u][2]
                pick = onehotT[:, DQ_COL[m] + c, 0:r]
                pe.wait_ge(q4_done, u + 1)
                if j >= BANKS:
                    pe.wait_ge(mul_done, j - BANKS + 1)
                pe.matmul(psum[0:r, 0, j % BANKS, 0:n], identb[0:r, 0:r], q4[0:r, u % 2, at:at + n], start=True, stop=False)
                pe.matmul(psum[0:r, 0, j % BANKS, 0:n], hi(pick[0:G_ROWS]), hi(ztab[:, a:a + n]), start=False, stop=True)
                pe.matmul(psum[0:r, 1, j % BANKS, 0:n], hi(pick), hi(stab[:, a:a + n]), start=True, stop=True).then_inc(picked, 1)


FB = B * S // HALF


def ffn_events():
    events = []
    for n in range(NT):
        events.append(("gu", n))
        if n in (3, 5, 7, 9):
            events.append(("xt", (n - 3) // 2))
        if n >= 1:
            events.append(("down", n - 1))
    return events + [("down", NT - 1)]


F_USES = {e: n for n, e in enumerate(e for e in ffn_events() if e[0] != "down")}
F_PER = len(F_USES)


def ffn(nc, x1_dram, xin, x_in, ident, gu, wd, x2_dram, next_loads, next_in):
    with ExitStack() as ctx:
        def sb(name, shape, dt=F32):
            return ctx.enter_context(nc.sbuf_tensor(name, shape, dt))

        def sem(name):
            return ctx.enter_context(nc.semaphore(name))

        half_neg = sb("f_half_neg", [P, 4])
        xsum = sb("f_xsum", [P, 4, D])
        xT = [[sb(f"f_xT{r}{i}", [P, DC, HALF]) for i in range(2)] for r in range(2)]
        h = sb("f_h", [P, 2, HALF])
        h_parts = [sb(f"f_h_part{i}", [P, 2, HALF]) for i in range(2)]
        stats = sb("f_stats", [P, 4, 6])
        moments = sb("f_moments", [P, 4, 2])
        rstd = sb("f_rstd", [P, 4])
        ystats = sb("f_ystats", [P, 4, 6])
        ymom = sb("f_ymom", [P, 4, 2])
        yrstd = sb("f_yrstd", [P, 4])
        yshift = sb("f_yshift", [P, 4])

        pair = ctx.enter_context(nc.psum_tensor("f_pair", [P, 2, 2, 512], F32))
        Y = ctx.enter_context(nc.psum_tensor("f_Y", [P, 4, 512], F32))

        init = sem("f_init")
        waited = sem("f_waited")
        res_in = sem("f_res_in")
        pair_full = sem("f_pair_full")
        pair_free = sem("f_pair_free")
        dve = sem("f_dve")
        var_done = sem("f_var_done")
        rstd_done = sem("f_rstd_done")
        xn_ready = sem("f_xn_ready")
        xthi = sem("f_xthi")
        sil_done = sem("f_sil_done")
        h_ready = sem("f_h_ready")
        h_hi = sem("f_h_hi")
        h_lo = sem("f_h_lo")
        y_tile = sem("f_y_tile")
        down_done = sem("f_down_done")
        y_var = sem("f_y_var")
        y_rstd = sem("f_y_rstd")
        shift_done = sem("f_shift_done")
        y_ready = sem("f_y_ready")
        x2_ready = sem("f_x2_ready")
        x2_out = sem("f_x2_out")

        block = ctx.enter_context(nc.Block())

        def number(blk, e):
            return blk * F_PER + (4 + F_USES[e])

        def pair_of(r, e):
            return pair[:, (4 + r * F_PER + F_USES[e]) % 2, :, :]

        def rows(dram, row):
            return dram[bass.ds(row, HALF), :].rearrange("(t p) d -> p t d", p=P)

        @block.sync
        def _(sp):
            for dst, src in next_loads:
                sp.dma_start(dst[:], src.rearrange("(c p) n -> p c n", p=P)).then_inc(next_in, 16)
            sp.sem_inc(x2_out, 16)
            with sp.Fori(0, FB // 2) as it:
                first, second = sp.snap(it * (2 * HALF)), sp.snap(it * (2 * HALF) + HALF)
                third = 2 * HALF
                for r, here, after in ((0, first, second), (1, second, third)):
                    blk = it * 2 + r
                    sp.wait_ge(pair_full, blk * F_PER + 4)
                    sp.dma_start(xin[:, :, :], rows(x1_dram, after)).then_inc(x_in, 16)
                    sp.wait_ge(x2_out, blk * 16 + 16)
                    sp.dma_start(xsum[:, :, :], rows(x1_dram, here)).then_inc(res_in, 16)
                    sp.wait_ge(x2_ready, blk * 4 + 8)
                    sp.dma_start(rows(x2_dram, here), xsum[:, :, :]).then_inc(x2_out, 16)
            sp.wait_ge(x2_out, 16 * FB + 16)
            sp.wait_ge(x_in, 16 * (FB + 1))

        @block.gpsimd
        def _(pool):
            pool.memset(half_neg[:, :], -0.5).then_inc(init, 1)
            pool.sem_inc(h_lo, 2)
            pool.wait_ge(init, 1)

            def block_rstd(k):
                pool.wait_ge(var_done, k + 1)
                pool.tensor_tensor(rstd[:, :], moments[:, :, 1], half_neg[:, :], ALU.pow).then_inc(rstd_done, 1)

            block_rstd(0)
            with pool.Fori(0, FB // 2) as it:
                for r in range(2):
                    blk = it * 2 + r
                    for n in range(NT):
                        if n == 2:
                            block_rstd(blk + 1)
                        w, slot = tile_w(n), (r * NT + n) % 2
                        pool.wait_ge(h_hi, blk * NT + n + 1)
                        pool.tensor_tensor(hi(h_parts[1][0:w, slot, :]), h[0:w, slot, :], h_parts[0][0:w, slot, :],
                                           ALU.subtract).then_inc(h_lo, 1)
                    pool.wait_ge(y_var, blk + 1)
                    pool.tensor_tensor(yrstd[:, :], ymom[:, :, 1], half_neg[:, :], ALU.pow).then_inc(y_rstd, 1)

        @block.scalar
        def _(act):
            def xt_hi(ring, t, src):
                act.activation(hi(xT[ring][0][:, :, t * P:(t + 1) * P]), src.rearrange("p (c q) -> p c q", c=DC), ACT.Copy).then_inc(xthi, 1)

            for t in range(4):
                act.wait_ge(pair_full, t + 1)
                xt_hi(0, t, pair[:, t % 2, 0, :])
            with act.Fori(0, FB // 2) as it:
                for r in range(2):
                    blk = it * 2 + r
                    for kind, n in ffn_events():
                        if kind == "down":
                            continue
                        src = pair_of(r, (kind, n))
                        act.wait_ge(pair_full, number(blk, (kind, n)) + 1)
                        if kind == "xt":
                            xt_hi(1 - r, n, src[:, 0, :])
                            continue
                        w, slot = tile_w(n), (r * NT + n) % 2
                        act.wait_ge(h_lo, blk * NT + n + 1)
                        act.activation(h[0:w, slot, :], src[0:w, 0, :], ACT.Silu).then_inc(sil_done, 1)
                        act.wait_ge(h_ready, blk * NT + n + 2)
                        act.wait_ge(down_done, blk * NT + n + 1)
                        act.activation(hi(h_parts[0][0:w, slot, :]), h[0:w, slot, :], ACT.Copy).then_inc(h_hi, 1)

        @block.vector
        def _(v):
            v.sem_inc(pair_free, 2)
            v.sem_inc(h_ready, 1)
            v.sem_inc(y_ready, 4)
            v.sem_inc(x2_ready, 4)

            def row_moments(k, base):
                v.wait_ge(x_in, k * 16 + 16)
                v.sem_inc(waited, 1)
                for t in range(4):
                    v.bn_stats(stats[:, t, :], xin[:, t, :]).then_inc(dve, 1)
                v.wait_ge(dve, base + 4)
                v.sem_inc(waited, 1)
                for t in range(4):
                    v.bn_aggr(moments[:, t, :], stats[:, t, :]).then_inc(dve, 1)
                v.wait_ge(dve, base + 8)
                v.tensor_scalar(moments[:, :, 1], moments[:, :, 1], EPS, None, ALU.add).then_inc(var_done, 1)

            def normalize(k):
                v.wait_ge(rstd_done, k + 1)
                for t in range(4):
                    v.tensor_scalar(xin[:, t, :], xin[:, t, :], moments[:, t, 0:1], rstd[:, t:t + 1], ALU.subtract, ALU.mult).then_inc(xn_ready, 1)

            def xt_lo(ring, t, src, n):
                v.wait_ge(xthi, n + 1)
                at = slice(t * P, (t + 1) * P)
                v.tensor_tensor(hi(xT[ring][1][:, :, at]), src.rearrange("p (c q) -> p c q", c=DC), xT[ring][0][:, :, at],
                                ALU.subtract).then_inc(pair_free, 1)

            row_moments(0, 0)
            normalize(0)
            for t in range(4):
                v.wait_ge(pair_full, t + 1)
                xt_lo(0, t, pair[:, t % 2, 0, :], t)
            with v.Fori(0, FB // 2) as it:
                for r in range(2):
                    blk = it * 2 + r
                    base = blk * 16 + 8
                    for kind, n in ffn_events():
                        if kind == "down":
                            continue
                        src = pair_of(r, (kind, n))
                        v.wait_ge(pair_full, number(blk, (kind, n)) + 1)
                        if kind == "xt":
                            xt_lo(1 - r, n, src[:, 0, :], blk * 4 + n + 4)
                            continue
                        w, slot = tile_w(n), (r * NT + n) % 2
                        v.wait_ge(sil_done, blk * NT + n + 1)
                        v.tensor_tensor(h[0:w, slot, :], h[0:w, slot, :], src[0:w, 1, :], ALU.mult).then_inc(h_ready, 1)
                        v.wait_ge(h_ready, blk * NT + n + 2)
                        v.sem_inc(pair_free, 1)
                        if n == 1:
                            row_moments(blk + 1, base)
                        if n == 2:
                            normalize(blk + 1)
                    for t in range(4):
                        if t < 3:
                            v.wait_ge(y_tile, blk * 3 + t + 1)
                        else:
                            v.wait_ge(down_done, blk * NT + NT + 2)
                        v.sem_inc(waited, 1)
                        v.bn_stats(ystats[:, t, :], Y[:, t, :]).then_inc(dve, 1)
                    v.wait_ge(dve, base + 12)
                    v.sem_inc(waited, 1)
                    for t in range(4):
                        v.bn_aggr(ymom[:, t, :], ystats[:, t, :]).then_inc(dve, 1)
                    v.wait_ge(dve, base + 16)
                    v.tensor_scalar(ymom[:, :, 1], ymom[:, :, 1], EPS, None, ALU.add).then_inc(y_var, 1)
                    v.wait_ge(y_rstd, blk + 1)
                    v.scalar_tensor_tensor(yshift[:, :], ymom[:, :, 0], -1.0, yrstd[:, :], ALU.mult, ALU.mult).then_inc(shift_done, 1)
                    v.wait_ge(res_in, blk * 16 + 16)
                    for t in range(4):
                        v.scalar_tensor_tensor(xsum[:, t, :], Y[:, t, :], yrstd[:, t:t + 1], xsum[:, t, :], ALU.mult, ALU.add).then_inc(y_ready, 1)
                    v.wait_ge(shift_done, blk + 1)
                    for t in range(4):
                        v.wait_ge(y_ready, blk * 4 + t + 5)
                        v.tensor_scalar(xsum[:, t, :], xsum[:, t, :], yshift[:, t:t + 1], None, ALU.add).then_inc(x2_ready, 1)

        @block.tensor
        def _(pe):
            pe.sem_inc(down_done, 2)

            def transposes(dst, t):
                for c in range(DC):
                    last = pe.transpose(dst[:, c * P:(c + 1) * P], xin[:, t, c * P:(c + 1) * P], ident[:, :])
                last.then_inc(pair_full, 1)

            for t in range(4):
                pe.wait_ge(pair_free, t + 1)
                pe.wait_ge(xn_ready, t + 1)
                transposes(pair[:, t % 2, 0, :], t)
            with pe.Fori(0, FB // 2) as it:
                for r in range(2):
                    blk = it * 2 + r
                    for kind, n in ffn_events():
                        w, slot = tile_w(n), (r * NT + n) % 2
                        if kind == "down":
                            pe.wait_ge(h_lo, blk * NT + n + 3)
                            if n == 0:
                                pe.wait_ge(y_ready, blk * 4 + 4)
                            for t in range(4):
                                at = slice(t * P, (t + 1) * P)
                                pe.matmul(Y[:, t, :], hi(h_parts[0][0:w, slot, at]), hi(wd[0][0:w, n, :]), start=(n == 0), stop=False)
                                pe.matmul(Y[:, t, :], hi(h_parts[0][0:w, slot, at]), hi(wd[1][0:w, n, :]), start=False, stop=False)
                                last = pe.matmul(Y[:, t, :], hi(h_parts[1][0:w, slot, at]), hi(wd[0][0:w, n, :]), start=False, stop=(n == NT - 1))
                                if n == NT - 1 and t < 3:
                                    last.then_inc(y_tile, 1)
                            last.then_inc(down_done, 1)
                            continue
                        dst = pair_of(r, (kind, n))
                        pe.wait_ge(pair_free, number(blk, (kind, n)) + (2 if (kind, n) == ("gu", 0) else 1))
                        if kind == "xt":
                            pe.wait_ge(xn_ready, blk * 4 + n + 5)
                            transposes(dst[:, 0, :], n)
                            continue
                        at = slice(n * P, n * P + w)
                        for m in range(2):
                            last = three_pass(pe, dst[0:w, m, :], lambda c: hi(gu[0][:, m, c, at]), lambda c: hi(gu[1][:, m, c, at]),
                                              lambda c: hi(xT[r][0][:, c, :]), lambda c: hi(xT[r][1][:, c, :]), DC)
                        last.then_inc(pair_full, 1)



BLK = 32
RA, RB, NE = 32, 8, 3
R = RA + RB
SCALING = 16.0 / 32.0


DUO = 2 * P
DUOS = 4
L_STEPS = 2 * DUOS
GROUPS = B * S // (DUOS * DUO)


def layer1(nc, x2_dram, wa, mi, ahead_in, b_attn, w_base, b_base, enc, coefs, cmasks, ident, blockones_d, gmask_d, fourier_d, out_dram):
    with ExitStack() as ctx:
        def sb(name, shape, dt=F32):
            return ctx.enter_context(nc.sbuf_tensor(name, shape, dt))

        def sem(name):
            return ctx.enter_context(nc.semaphore(name))

        half_neg = sb("l_half_neg", [P, 2])
        minus_one = sb("l_minus_one", [P, 2])
        ones = sb("l_ones", [2, P])
        x = sb("l_x", [P, DUOS, 2, D])
        xout = sb("l_xout", [P, 2, 2, D])
        xn = sb("l_xn", [P, 2, 2, D])
        xT = [sb(f"l_xT{i}", [P, 2, 2, DC, P]) for i in range(2)]
        yn = sb("l_yn", [P, 2, 2, D])
        stats = sb("l_stats", [P, 2, 2, 2, 6])
        mom = sb("l_mom", [P, 2, 2, 2, 2])
        neg_mean = sb("l_neg_mean", [P, 2, 2, 2])
        rstd = sb("l_rstd", [P, 2, 2, 2])
        shift = sb("l_shift", [P, 2, 2, 2])
        wT = [[sb(f"l_wT{l}{i}", [P, DC, D]) for i in range(2)] for l in range(2)]
        bias = [sb(f"l_bias{l}", [2, D]) for l in range(2)]
        blockones = sb("l_blockones", [P, P])
        gmask = sb("l_gmask", [P, 3])
        fourier = sb("l_fourier", [P, DC, D])
        wb = sb("l_wb", [P, DC, D])
        msum = sb("l_msum", [P, DC * D // BLK])
        on = sb("l_on", [P, DC * D // BLK])
        wm = sb("l_wm", [P, DC, D])
        ca = sb("l_ca", [P, NE, DC, RA])
        cb = sb("l_cb", [P, NE, DC, RB])
        ka = sb("l_ka", [P, NE, DC, RA], U8)
        kb = sb("l_kb", [P, NE, DC, RB], U8)
        cm = sb("l_cm", [P, NE, DC, R])
        csum = sb("l_csum", [P, 2, DC, R])
        E = sb("l_E", [R, D])
        M = sb("l_M", [R, D])
        wbT = sb("l_wbT", [P, DC, D])
        wsum = sb("l_wsum", [P, DC, D])
        braw = sb("l_braw", [2, 2, D])
        bhi = sb("l_bhi", [2, 2, D])
        psum = ctx.enter_context(nc.psum_tensor("l_psum", [P, 8, 512], F32))
        turn = psum[:, 0:4, :].rearrange("p (s t) k -> p s t k", s=2)
        prod = psum[:, 4:8, :].rearrange("p (s t) k -> p s t k", s=2)
        COUNT, MID, DELTA, BASE = 2, 3, 4, 6

        blockones_in = sem("l_blockones_in")
        bias_in = sem("l_bias_in")
        coefs_in = sem("l_coefs_in")
        wb_in = sem("l_wb_in")
        chain = sem("l_chain")
        mask_ready = sem("l_mask_ready")
        count_done = sem("l_count_done")
        wm_ready = sem("l_wm_ready")
        a_turned = sem("l_a_turned")
        csum_ready = sem("l_csum_ready")
        M_done = sem("l_M_done")
        M_ready = sem("l_M_ready")
        delta_done = sem("l_delta_done")
        b_turned = sem("l_b_turned")
        wbT_ready = sem("l_wbT_ready")
        wsum_ready = sem("l_wsum_ready")
        wT_hi = sem("l_wT_hi")
        wT_lo = sem("l_wT_lo")
        b_ready = sem("l_b_ready")
        init = sem("l_init")
        ones_set = sem("l_ones_set")
        waited = sem("l_waited")
        x_in = [sem(f"l_x_in{d}") for d in range(DUOS)]
        dve = sem("l_dve")
        pool_chain = sem("l_pool_chain")
        var_x = sem("l_var_x")
        shift_x = sem("l_shift_x")
        xn_ready = sem("l_xn_ready")
        turned = sem("l_turned")
        xthi = sem("l_xthi")
        xtlo = sem("l_xtlo")
        y_done = sem("l_y_done")
        var_y = sem("l_var_y")
        shift_y = sem("l_shift_y")
        yn_ready = sem("l_yn_ready")
        sum_done = sem("l_sum_done")
        x_out = [sem(f"l_x_out{i}") for i in range(2)]

        block = ctx.enter_context(nc.Block())

        COEFS = 4 + 3

        def chunks(w):
            return w.rearrange("(c p) n -> p c n", p=P)

        def rows(dram, row):
            return dram[bass.ds(row, DUO), :].rearrange("(t p) d -> p t d", p=P)

        @block.sync
        def _(sp):
            def load_x(d):
                sp.dma_start(x[:, d], rows(x2_dram, d * DUO)).then_inc(x_in[d], 16)

            sp.dma_start(blockones[:], blockones_d).then_inc(blockones_in, 16)
            sp.dma_start(gmask[:], gmask_d).then_inc(bias_in, 16)
            for l, b in enumerate((b_attn, b_base)):
                sp.dma_start(braw[:, l, :], b.partition_broadcast(2)).then_inc(bias_in, 16)
            load_x(0)
            load_x(1)
            for dst, src in ((ca, coefs[0]), (cb, coefs[1]), (ka, cmasks[0]), (kb, cmasks[1])):
                sp.dma_start(dst[:].rearrange("p e c r -> p (e c) r"), src.rearrange("e (c p) r -> p (e c) r", p=P)).then_inc(coefs_in, 16)
            sp.dma_start(E[0:RA, :], enc[0]).then_inc(coefs_in, 16)
            sp.dma_start(E[RA:R, :], enc[1]).then_inc(coefs_in, 16)
            sp.dma_start(fourier[:], chunks(fourier_d)).then_inc(coefs_in, 16)
            sp.dma_start(wb[:], chunks(w_base)).then_inc(wb_in, 16)
            load_x(2)
            load_x(3)
            for i in range(2):
                sp.sem_inc(x_out[i], 16)
            with sp.Fori(0, GROUPS) as g:
                here = [sp.snap(g * (DUOS * DUO) + d * DUO) for d in range(DUOS)]
                for d in range(DUOS):
                    sp.wait_ge(sum_done, g * (2 * L_STEPS) + 2 * (DUOS + d) + 6)
                    sp.dma_start(x[:, d], rows(x2_dram, (DUOS + d) * DUO)).then_inc(x_in[d], 16)
                    sp.dma_start(rows(out_dram, here[d]), xout[:, d % 2]).then_inc(x_out[d % 2], 16)
            for i in range(2):
                sp.wait_ge(x_out[i], 16 * GROUPS * DUOS // 2 + 16)
            for d in range(DUOS):
                sp.wait_ge(x_in[d], 16 * (GROUPS + 1))

        @block.gpsimd
        def _(pool):
            pool.memset(half_neg[:, :], -0.5).then_inc(init, 1)
            pool.memset(minus_one[:, :], -1.0).then_inc(init, 1)
            pool.sem_inc(sum_done, 4)
            pool.wait_ge(init, 2)

            def scale_shift(which, g, k, var, done, links):
                s = k % 2
                pool.wait_ge(var, g * L_STEPS + k + 1)
                pool.tensor_tensor(neg_mean[:, which, s, :], mom[:, which, s, :, 0], minus_one[:, :], ALU.mult).then_inc(pool_chain, 1)
                pool.tensor_tensor(rstd[:, which, s, :], mom[:, which, s, :, 1], half_neg[:, :], ALU.pow).then_inc(pool_chain, 1)
                pool.wait_ge(pool_chain, g * (4 * L_STEPS) + links)
                pool.tensor_tensor(shift[:, which, s, :], neg_mean[:, which, s, :], rstd[:, which, s, :], ALU.mult).then_inc(done, 1)

            for k in range(2):
                scale_shift(0, 0, k, var_x, shift_x, 2 * k + 2)
            with pool.Fori(0, GROUPS) as g:
                for k in range(L_STEPS):
                    scale_shift(0, g, k + 2, var_x, shift_x, 4 * k + 6)
                    scale_shift(1, g, k, var_y, shift_y, 4 * k + 8)
                    d = k % DUOS
                    if k >= DUOS:
                        pool.wait_ge(x_out[d % 2], g * (16 * DUOS // 2) + 16 * (d // 2) + 16)
                    for t in range(2):
                        pool.wait_ge(yn_ready, g * (2 * L_STEPS) + 2 * k + t + 5)
                        dst = x[:, d, t, :] if k < DUOS else xout[:, d % 2, t, :]
                        pool.tensor_tensor(dst, x[:, d, t, :], yn[:, k % 2, t, :], ALU.add).then_inc(sum_done, 1)

        @block.vector
        def _(v):
            v.sem_inc(xtlo, 4)

            def moments(which, k, src, var, linked):
                s = k % 2
                for t in range(2):
                    v.bn_stats(stats[:, which, s, t, :], src(t)).then_inc(dve, 1)
                v.wait_ge(dve, linked - 2)
                v.sem_inc(waited, 1)
                for t in range(2):
                    v.bn_aggr(mom[:, which, s, t, :], stats[:, which, s, t, :]).then_inc(dve, 1)
                v.wait_ge(dve, linked)
                v.tensor_scalar(mom[:, which, s, :, 1], mom[:, which, s, :, 1], EPS, None, ALU.add).then_inc(var, 1)

            def row_moments(g, k, linked):
                d = k % DUOS
                if k % L_STEPS < DUOS:
                    v.wait_ge(x_in[d], g * 16 + 16 * (k // L_STEPS) + 16)
                else:
                    v.wait_ge(sum_done, g * (2 * L_STEPS) + 2 * (k - DUOS) + 6)
                v.sem_inc(waited, 1)
                moments(0, k, lambda t: x[:, d, t, :], var_x, linked)

            def low_parts(g, k):
                for t in range(2):
                    v.wait_ge(xthi, g * (2 * L_STEPS) + 2 * k + t + 1)
                    v.tensor_tensor(hi(xT[1][:, k % 2, t]), turn[:, k % 2, t, :].rearrange("p (c q) -> p c q", c=DC), xT[0][:, k % 2, t],
                                    ALU.subtract).then_inc(xtlo, 1)

            v.memset(ones[:, :], 1.0).then_inc(ones_set, 1)
            n_chain = [0]

            def link(ins):
                n_chain[0] += 1
                ins.then_inc(chain, 1)
                v.wait_ge(chain, n_chain[0])

            v.wait_ge(ahead_in, 32)
            v.tensor_reduce(msum[:, :], mi[:, :, :].rearrange("p c (k w) -> p (c k) w", w=BLK), AX.X, ALU.add).then_inc(mask_ready, 1)
            v.wait_ge(count_done, 1)
            link(v.tensor_scalar(on[:, :], psum[:, COUNT, 0:DC * D // BLK], 0.0, None, ALU.is_gt))
            for c in range(DC):
                v.tensor_tensor(wm[:, c, :].rearrange("p (k w) -> p k w", w=BLK), wa[:, c, :].rearrange("p (k w) -> p k w", w=BLK),
                                on[:, c * D // BLK:(c + 1) * D // BLK].unsqueeze(2).to_broadcast([P, D // BLK, BLK]), ALU.mult).then_inc(wm_ready, 1)
            v.wait_ge(bias_in, 16 * 3)
            link(v.tensor_copy(hi(bhi[:]), braw[:]))
            for l in range(2):
                v.scalar_tensor_tensor(hi(bias[l][:, :]), bhi[:, l, :], gmask[0:2, 2:3], braw[:, l, :], ALU.mult, ALU.add).then_inc(b_ready, 1)
            row_moments(0, 0, 4)
            for c in range(DC):
                v.wait_ge(wT_hi, c + 1)
                v.tensor_tensor(hi(wT[0][1][:, c, :]), psum[:, 4 + c, :], wT[0][0][:, c, :], ALU.subtract).then_inc(wT_lo, 1)
            row_moments(0, 1, 8)
            v.wait_ge(coefs_in, 16 * COEFS)
            link(v.tensor_tensor(cm[:, :, :, 0:RA].rearrange("p e c r -> p (e c) r"), ca[:].rearrange("p e c r -> p (e c) r"),
                                 ka[:].rearrange("p e c r -> p (e c) r"), ALU.mult))
            link(v.tensor_tensor(cm[:, :, :, RA:R].rearrange("p e c r -> p (e c) r"), cb[:].rearrange("p e c r -> p (e c) r"),
                                 kb[:].rearrange("p e c r -> p (e c) r"), ALU.mult))
            link(v.tensor_tensor(csum[:, 0], cm[:, 0], cm[:, 1], ALU.add))
            v.tensor_tensor(csum[:, 1], csum[:, 0], cm[:, 2], ALU.add).then_inc(csum_ready, 1)
            low_parts(0, 0)
            v.wait_ge(M_done, 1)
            v.tensor_scalar(M[:, :], psum[0:R, MID, :], SCALING, None, ALU.mult).then_inc(M_ready, 1)
            for c in range(DC + 1):
                if c < DC:
                    v.wait_ge(delta_done, c + 1)
                    v.wait_ge(wbT_ready, c + 1)
                    v.tensor_tensor(wsum[:, c, :], psum[:, DELTA + c % 2, :], wbT[:, c, :], ALU.add).then_inc(wsum_ready, 1)
                if c:
                    v.wait_ge(wT_hi, DC + c)
                    v.tensor_tensor(hi(wT[1][1][:, c - 1, :]), wsum[:, c - 1, :], wT[1][0][:, c - 1, :], ALU.subtract).then_inc(wT_lo, 1)
            with v.Fori(0, GROUPS) as g:
                for k in range(L_STEPS):
                    linked = g * (8 * L_STEPS) + 8 * k + 8
                    v.wait_ge(xn_ready, g * (2 * L_STEPS) + 2 * k + 2)
                    v.sem_inc(waited, 1)
                    row_moments(g, k + 2, linked + 4)
                    low_parts(g, k + 1)
                    v.wait_ge(y_done, g * (2 * L_STEPS) + 2 * k + 6)
                    v.sem_inc(waited, 1)
                    moments(1, k, lambda t: prod[:, k % 2, t, :], var_y, linked + 8)

        @block.scalar
        def _(act):
            act.sem_inc(yn_ready, 4)

            def normalize(g, k):
                act.wait_ge(shift_x, g * L_STEPS + k + 1)
                act.wait_ge(turned, g * (2 * L_STEPS) + 2 * k + 2)
                act.sem_inc(waited, 1)
                for t in range(2):
                    act.activation(xn[:, k % 2, t, :], x[:, k % DUOS, t, :], ACT.Identity, bias=shift[:, 0, k % 2, t:t + 1],
                                   scale=rstd[:, 0, k % 2, t:t + 1]).then_inc(xn_ready, 1)

            def high_parts(g, k):
                act.wait_ge(y_done, g * (2 * L_STEPS) + 2 * k + 2)
                for t in range(2):
                    act.wait_ge(turned, g * (2 * L_STEPS) + 2 * k + t + 5)
                    act.activation(hi(xT[0][:, k % 2, t]), turn[:, k % 2, t, :].rearrange("p (c q) -> p c q", c=DC), ACT.Copy).then_inc(xthi, 1)

            for c in range(DC):
                act.wait_ge(a_turned, c + 1)
                act.activation(hi(wT[0][0][:, c, :]), psum[:, 4 + c, :], ACT.Copy).then_inc(wT_hi, 1)
            normalize(0, 0)
            normalize(0, 1)
            high_parts(0, 0)
            for c in range(DC + 1):
                if c < DC:
                    act.wait_ge(b_turned, c + 1)
                    act.activation(wbT[:, c, :], psum[:, BASE + c % 2, :], ACT.Copy).then_inc(wbT_ready, 1)
                if c:
                    act.wait_ge(wsum_ready, c)
                    act.activation(hi(wT[1][0][:, c - 1, :]), wsum[:, c - 1, :], ACT.Copy).then_inc(wT_hi, 1)
            with act.Fori(0, GROUPS) as g:
                for k in range(L_STEPS):
                    high_parts(g, k + 1)
                    normalize(g, k + 2)
                    act.wait_ge(shift_y, g * L_STEPS + k + 1)
                    act.wait_ge(sum_done, g * (2 * L_STEPS) + 2 * k + 2)
                    act.sem_inc(waited, 1)
                    for t in range(2):
                        act.activation(yn[:, k % 2, t, :], prod[:, k % 2, t, :], ACT.Identity, bias=shift[:, 1, k % 2, t:t + 1],
                                       scale=rstd[:, 1, k % 2, t:t + 1]).then_inc(yn_ready, 1)

        @block.tensor
        def _(pe):
            pe.sem_inc(turned, 4)
            pe.sem_inc(y_done, 4)
            def transposes(g, k):
                pe.wait_ge(xtlo, g * (2 * L_STEPS) + 2 * k + 2)
                for t in range(2):
                    pe.wait_ge(xn_ready, g * (2 * L_STEPS) + 2 * k + t + 1)
                    for c in range(DC):
                        last = pe.transpose(turn[:, k % 2, t, c * P:(c + 1) * P], xn[:, k % 2, t, c * P:(c + 1) * P], ident[:, :])
                    last.then_inc(turned, 1)

            pe.wait_ge(blockones_in, 16)
            pe.wait_ge(mask_ready, 1)
            pe.matmul(psum[:, COUNT, 0:DC * D // BLK], blockones[:, :], msum[:, :], start=True, stop=True).then_inc(count_done, 1)
            pe.wait_ge(wm_ready, DC)
            for c in range(DC):
                for n in range(DC):
                    last = pe.transpose(psum[:, 4 + c, n * P:(n + 1) * P], wm[:, n, c * P:(c + 1) * P], ident[:, :])
                last.then_inc(a_turned, 1)
            transposes(0, 0)
            pe.wait_ge(csum_ready, 1)
            for c in range(DC):
                last = pe.matmul(psum[0:R, MID, :], csum[:, 1, c, :], fourier[:, c, :], start=(c == 0), stop=(c == DC - 1))
            last.then_inc(M_done, 1)
            pe.wait_ge(wT_lo, DC)
            pe.wait_ge(wb_in, 16)
            for c in range(DC):
                if c >= 2:
                    pe.wait_ge(wbT_ready, c - 1)
                for n in range(DC):
                    last = pe.transpose(psum[:, BASE + c % 2, n * P:(n + 1) * P], wb[:, n, c * P:(c + 1) * P], ident[:, :])
                last.then_inc(b_turned, 1)
                if c == 0:
                    pe.wait_ge(M_ready, 1)
                if c >= 2:
                    pe.wait_ge(wsum_ready, c - 1)
                pe.matmul(psum[:, DELTA + c % 2, :], E[:, c * P:(c + 1) * P], M[:, :], start=True, stop=True).then_inc(delta_done, 1)
            pe.wait_ge(wsum_ready, DC)
            pe.wait_ge(ones_set, 1)
            pe.wait_ge(b_ready, 2)
            with pe.Fori(0, GROUPS) as g:
                for k in range(L_STEPS):
                    transposes(g, k + 1)
                    l = k // DUOS
                    if k == DUOS:
                        pe.wait_ge(wT_lo, 2 * DC)
                    pe.wait_ge(yn_ready, g * (2 * L_STEPS) + 2 * k + 2)
                    for t in range(2):
                        pe.wait_ge(xtlo, g * (2 * L_STEPS) + 2 * k + t + 5)
                        for c in range(DC):
                            pe.matmul(prod[:, k % 2, t, :], hi(xT[0][:, k % 2, t, c, :]), hi(wT[l][0][:, c, :]), start=(c == 0), stop=False)
                            pe.matmul(prod[:, k % 2, t, :], hi(xT[0][:, k % 2, t, c, :]), hi(wT[l][1][:, c, :]), start=False, stop=False)
                            pe.matmul(prod[:, k % 2, t, :], hi(xT[1][:, k % 2, t, c, :]), hi(wT[l][0][:, c, :]), start=False, stop=False)
                        pe.matmul(prod[:, k % 2, t, :], hi(ones[:, :]), hi(bias[l][:, :]), start=False, stop=True).then_inc(y_done, 1)


def program(nc, ins, outs):
    x = ins["L0_attn_hidden_states"].rearrange("b s d -> (b s) d")
    out = outs[0].rearrange("b s d -> (b s) d")
    x1 = nc.dram_tensor("x1_dram", (B * S, D), F32).ap()
    x2 = nc.dram_tensor("x2_dram", (B * S, D), F32).ap()
    q_scratch = nc.dram_tensor("q_scratch", (3, DC, P // HD, HD, HALF), BF16).ap()
    mats = [tuple(ins[f"L0_ffn_{m}_{k}"] for k in ("qweight", "scales", "qzeros", "g_idx")) for m in ("gate", "up", "down")]
    with ExitStack() as whole, nc.allow_low_precision(reason="float32r parts of exact splits"):
        def sb(name, shape, dt=F32):
            return whole.enter_context(nc.sbuf_tensor(name, shape, dt))

        ident = sb("ident", [P, P])
        identb = sb("identb", [P, P], BF16)
        shifts = sb("shifts", [P, 1], I32)
        group_ids = sb("group_ids", [P, 2 * G_ROWS + 1])
        gidx = sb("gidx", [P, DQ_COLS], I32)
        dq_in = whole.enter_context(nc.semaphore("dq_in"))
        dq_loads = group_index_loads(mats, gidx) + [(group_ids[:, :], ins["c_groups"]), (shifts[:, :], ins["c_shift"])]
        attention(nc, x, ins["L0_attn_Wqkv"], ins["L0_attn_Wo"], ins["c_ident"], ins["c_identb"], ins["c_mask"], ins["c_qrows"],
                  ins["c_krows"], ins["c_gmask"], q_scratch, x1, ident, identb, dq_loads, dq_in)
        wa = sb("l1_wa", [P, DC, D])
        mi = sb("l1_mask", [P, DC, D], I32)
        ahead_in = whole.enter_context(nc.semaphore("l1_ahead_in"))
        with ExitStack() as ctx:
            gu = [ctx.enter_context(nc.sbuf_tensor(f"gu{i}", [P, 2, DC, INTER], F32)) for i in range(2)]
            wd = [ctx.enter_context(nc.sbuf_tensor(f"wd{i}", [P, NT, D], F32)) for i in range(2)]
            xin = ctx.enter_context(nc.sbuf_tensor("f_xin", [P, 4, D], F32))
            x_in = ctx.enter_context(nc.semaphore("f_x_in"))
            dequantize(nc, mats, ident, identb, shifts, group_ids, gidx, (mi, wa), gu, wd,
                       [(xin[:, :, :], x1[0:HALF, :].rearrange("(t p) d -> p t d", p=P))], x_in)
            ffn(nc, x1, xin, x_in, ident, gu, wd, x2,
                ((mi, ins["L1_attn_mask"]), (wa, ins["L1_attn_weight"])), ahead_in)
        layer1(nc, x2, wa, mi, ahead_in, ins["L1_attn_bias"], ins["L1_ffn_W_base"], ins["L1_ffn_b_base"],
               (ins["L1_ffn_enc0"], ins["L1_ffn_enc1"]), (ins["L1_ffn_coefs0"], ins["L1_ffn_coefs1"]),
               (ins["L1_ffn_mask0"], ins["L1_ffn_mask1"]), ident, ins["c_blockones"], ins["c_gmask"], ins["c_fourier"], out)


def shape_constants(np):
    bf = np.dtype("bfloat16")

    def parts(a):
        p1 = a.astype(bf)
        p2 = (a - p1.astype(np.float32)).astype(bf)
        p3 = (a - p1.astype(np.float32) - p2.astype(np.float32)).astype(bf)
        return [p1, p2, p3]

    slope = (2.0 ** (-0.25)) ** np.arange(1, NH + 1, dtype=np.float64)
    slope = slope.astype(np.float32)
    q0 = -(np.arange(S) // P * P).astype(np.float32)
    ones = np.ones((NH, S), np.float32)
    qrows = np.zeros((POS_ROWS, NH, S), bf)
    krows = np.ones((POS_ROWS + 3, S), bf)
    for j, (s, sq) in enumerate(zip(parts(slope[:, None] * ones), parts((slope[:, None] * q0[None]).astype(np.float32)))):
        qrows[3 * j] = s
        qrows[3 * j + 1] = s
        qrows[3 * j + 2] = sq
        krows[3 * j] = (np.arange(S) // P * P).astype(bf)
        krows[3 * j + 1] = (np.arange(S) % P).astype(bf)
    gm = np.zeros((P, 3), np.float32)
    gm[1, 2] = -1.0
    for g, part in enumerate([0, 1, 2, 0, 1, 0]):
        gm[g * HD:(g + 1) * HD, 0] = -1.0 if part >= 1 else 0.0
        gm[g * HD:(g + 1) * HD, 1] = -1.0 if part >= 2 else 0.0
    q, k = np.arange(P)[:, None], np.arange(P)[None]
    mask = np.where(k > q, np.float32(-1e30), np.float32(0))
    t = np.arange(D, dtype=np.float64)[None, :]
    o = np.arange(D)[:, None]
    angle = 2.0 * np.pi * ((o + 1) // 2) * t / D
    fourier = np.sqrt(2.0 / D) * np.where(o % 2 == 1, np.cos(angle), np.sin(angle))
    fourier[0] = 1.0 / np.sqrt(D)
    fourier[D - 1] = np.cos(np.pi * t[0]) / np.sqrt(D)
    groups = np.zeros((P, 2 * G_ROWS + 1), np.float32)
    groups[:, 0:2 * G_ROWS] = np.arange(2 * G_ROWS) % G_ROWS
    groups[G_ROWS:2 * G_ROWS, 2 * G_ROWS] = -1.0
    return {
        "c_shift": (BITS * (np.arange(P, dtype=np.int32) % PACK))[:, None],
        "c_groups": groups,
        "c_blockones": np.kron(np.eye(P // BLK), np.ones((BLK, BLK))).astype(np.float32),
        "c_fourier": fourier.astype(np.float32),
        "c_ident": np.eye(P, dtype=np.float32),
        "c_identb": np.eye(P, dtype=np.float32).astype(bf),
        "c_mask": np.stack([np.tile(mask, (1, 4)), np.tile(mask.T, (1, 4))], 1).astype(bf),
        "c_qrows": qrows,
        "c_krows": krows,
        "c_gmask": gm,
    }


_INS = (['L0_attn_hidden_states', 'L0_attn_Wqkv', 'L0_attn_Wo']
        + [f'L0_ffn_{m}_{k}' for m in ('gate', 'up', 'down') for k in ('qweight', 'scales', 'qzeros', 'g_idx')]
        + ['L1_attn_mask', 'L1_attn_weight', 'L1_attn_bias', 'L1_ffn_W_base', 'L1_ffn_b_base', 'L1_ffn_enc0', 'L1_ffn_enc1',
           'L1_ffn_coefs0', 'L1_ffn_coefs1', 'L1_ffn_mask0', 'L1_ffn_mask1'])
_OUTS = [((B, S, D), 'float32')]


def kernel(**inputs):
    import numpy as _np
    import concourse.bacc as _bacc
    from concourse import mybir as _mybir
    from concourse.bass_utils import run_bass_kernel_spmd as _run

    nc = _bacc.Bacc("TRN2", target_bir_lowering=False, num_devices=1)
    arrays, ins, outs = {}, {}, []
    given = {name: _np.ascontiguousarray(inputs[name]) for name in _INS}
    given.update(shape_constants(_np))
    for name, a in given.items():
        arrays[f"in_{name}_dram"] = a
        ins[name] = nc.dram_tensor(f"in_{name}_dram", a.shape, _mybir.dt.from_np(a.dtype), kind="ExternalInput").ap()
    for i, (shape, dtype) in enumerate(_OUTS):
        dt = _mybir.dt.from_np(_np.dtype(dtype))
        outs.append(nc.dram_tensor(f"out_{i}_dram", shape, dt, kind="ExternalOutput").ap())
    program(nc, ins, outs)
    r = _run(nc, [arrays], core_ids=[0])
    got = tuple(r.results[0][f"out_{i}_dram"] for i in range(len(_OUTS)))
    return got[0]
```
